# Optimizing a Trainium2 kernel written in Bass

```python
import numpy as np
import jax
import jax.numpy as jnp

def _softmax(x, axis=-1):
    return jax.nn.softmax(x, axis=axis)

def _gelu(x):
    return jax.nn.gelu(x, approximate=True)

def _silu(x):
    return jax.nn.silu(x)

def _sigmoid(x):
    return jax.nn.sigmoid(x)

def _layernorm(x, axis=-1, eps=1e-05):
    m = jnp.mean(x, axis=axis, keepdims=True)
    v = jnp.var(x, axis=axis, keepdims=True)
    return (x - m) / jnp.sqrt(v + eps)

def _scatter_add(tgt, idx, src, axis=0):
    return tgt.at[idx].add(src)

def _segment_sum(src, seg, n):
    return jax.ops.segment_sum(src, seg, n)
kernel_name = 'mk_adj_resnorm_d2_adj_r2_883d06'

def setup_inputs(seed: int=0):
    np.random.seed(seed)
    _w = jnp.asarray

    def _rec_inputs():
        import jax
        import jax.numpy as jnp
        _gk = jax.random.key(seed)
        x = -0.0002928 + 1 * jax.random.normal(jax.random.fold_in(_gk, 1), (4096, 128), jnp.float32)
        _a = jax.random.bernoulli(jax.random.fold_in(_gk, 2), 0.000488281, (4096, 4096))
        _a = jnp.logical_or(_a, jnp.swapaxes(_a, -1, -2))
        _a = jnp.logical_or(_a, jnp.eye(4096, dtype=bool))
        adj = _a.astype(jnp.int32)
        return (x, adj)
    x, adj = _rec_inputs()

    def _L0_gnn_setup():
        import jax, jax.numpy as jnp
        import numpy as np
        N = 8192
        D = 128
        key = jax.random.key(seed)
        k1, k2, k3, k4 = jax.random.split(key, 4)
        x = jax.random.normal(k1, (N, D), dtype=jnp.float32)
        adj = jax.random.randint(k2, (N, N), 0, 2, dtype=jnp.int32)
        W = jax.random.normal(k3, (D, D), dtype=jnp.float32) * 0.05
        b = jax.random.normal(k4, (D,), dtype=jnp.float32) * 0.05
        return {'x': x, 'adj': adj, 'W': W, 'b': b}
    _L0_gnn_all = _L0_gnn_setup()
    _L0_gnn_in = {k: v for k, v in _L0_gnn_all.items() if k in ('W', 'b')}
    del _L0_gnn_all

    def _L1_gnn_setup():
        import jax, jax.numpy as jnp
        import numpy as np
        ALPHA = 0.2
        NEG_INF = -9000000000000000.0
        N, F_IN, F_OUT = (4096, 128, 128)
        key = jax.random.key(seed)
        k_h, k_adj, k_W, k_a = jax.random.split(key, 4)
        h = jax.random.normal(k_h, (N, F_IN), dtype=jnp.float32)
        adj = jax.random.randint(k_adj, (N, N), 0, 2, dtype=jnp.int32)
        gain = 1.414
        limit_W = gain * np.sqrt(6.0 / (F_IN + F_OUT))
        W = jax.random.uniform(k_W, (F_IN, F_OUT), dtype=jnp.float32, minval=-limit_W, maxval=limit_W)
        limit_a = gain * np.sqrt(6.0 / (2 * F_OUT + 1))
        a = jax.random.uniform(k_a, (2 * F_OUT, 1), dtype=jnp.float32, minval=-limit_a, maxval=limit_a)
        return {'h': h, 'adj': adj, 'W': W, 'a': a}
    _L1_gnn_all = _L1_gnn_setup()
    _L1_gnn_in = {k: v for k, v in _L1_gnn_all.items() if k in ('W', 'a')}
    del _L1_gnn_all
    return {'x': x, 'adj': adj, 'L0_gnn_W': _L0_gnn_in['W'], 'L0_gnn_b': _L0_gnn_in['b'], 'L1_gnn_W': _L1_gnn_in['W'], 'L1_gnn_a': _L1_gnn_in['a']}

def reference(x, adj, L0_gnn_W, L0_gnn_b, L1_gnn_W, L1_gnn_a):
    import jax
    import jax.numpy as jnp

    def _L0_gnn_ref(x, adj, W, b):
        import jax, jax.numpy as jnp
        import numpy as np
        N = 8192
        D = 128
        a = (adj == 1).astype(x.dtype)
        deg = jnp.sum(a, axis=1, keepdims=True)
        agg = jnp.einsum('ij,jf->if', a, x) / deg
        return agg @ W.T + b

    def _L1_gnn_ref(h, adj, W, a):
        import jax, jax.numpy as jnp
        import numpy as np
        ALPHA = 0.2
        NEG_INF = -9000000000000000.0
        N, F_IN, F_OUT = (4096, 128, 128)
        Wh = h @ W
        a1, a2 = (a[:F_OUT, 0], a[F_OUT:, 0])
        f1 = Wh @ a1
        f2 = Wh @ a2
        e = jax.nn.leaky_relu(f1[:, None] + f2[None, :], negative_slope=ALPHA)
        e = jnp.where(adj > 0, e, NEG_INF)
        attention = jax.nn.softmax(e, axis=1)
        h_prime = attention @ Wh
        return jax.nn.elu(h_prime)
    x = _layernorm(x + _L0_gnn_ref(x, adj, L0_gnn_W, L0_gnn_b), axis=-1)
    x = _layernorm(x + _L1_gnn_ref(x, adj, L1_gnn_W, L1_gnn_a), axis=-1)
    return x

_drawn_inputs = setup_inputs


def setup_inputs(seed=0):
    import zlib

    import numpy as np

    out = dict(_drawn_inputs(seed))
    spreads = {}
    factors = {}
    for name, (base, spread) in spreads.items():
        noise = np.random.default_rng([zlib.crc32(name.encode()), seed]).standard_normal(out[name].shape)
        drawn = base * np.exp(spread * noise) if base else spread * noise
        out[name] = jnp.asarray(drawn.astype(out[name].dtype))
    for name, factor in factors.items():
        out[name] = (out[name] * factor).astype(out[name].dtype)
    return out
```

```python
from contextlib import ExitStack

import concourse.bass as bass
from concourse import mybir

ALU = mybir.AluOpType
ACT = mybir.ActivationFunctionType
AX = mybir.AxisListType
F32, BF16, F16 = mybir.dt.float32, mybir.dt.bfloat16, mybir.dt.float16
I32, I8 = mybir.dt.int32, mybir.dt.int8

P = 128
N = 4096
F = 128
NT = N // P
GI = 512
NG = N // GI
IT = GI // P
CJ = 2
NC = NT // CJ
SLOTS = 4
XW = 3 * F + 1
HW = F + 1
VW = 2 * HW
RING = 4
EPS = 1e-5
ALPHA = 0.2
EXP_BITS = 0x7F800000
MAN_BITS = 0x007FFFFF
BITS_64 = 0x42800000


def build(nc, x_tiles, adj_tiles, w0t, b0, w1, w1t, a_cols, out_tiles):
    ctx = ExitStack()
    with ctx:
        def sb(name, shape, dt):
            return ctx.enter_context(nc.sbuf_tensor(name, shape, dt))

        def sem(name):
            return ctx.enter_context(nc.semaphore(name))

        x1_dram = nc.dram_tensor("x1_scratch", [NG, P, IT * F], F32, kind="Internal").ap()
        f1_dram = nc.dram_tensor("f1_scratch", [NG, 1, GI], F32, kind="Internal").ap()
        v_dram = nc.dram_tensor("v_scratch", [NG, P, IT * 2 * VW], F16, kind="Internal").ap()

        mask = sb("mask", [P, NG, NT * GI], I8)
        first_arena = sb("first_arena", [P, NT * XW + SLOTS * CJ * GI * 2], BF16)
        second_arena = sb("second_arena", [P, 10304], BF16)
        xparts = first_arena[:, 0:NT * XW].rearrange("p (t c) -> p t c", t=NT)
        adj_in = first_arena[:, NT * XW:].bitcast(I32).rearrange("p (s c) -> p s c", s=SLOTS)
        a01 = second_arena[:, 0:SLOTS * CJ * GI].rearrange("p (s c) -> p s c", s=SLOTS)
        mid_at = SLOTS * CJ * GI

        def mid(n, width=IT * F):
            return second_arena[:, mid_at + 1032 * n:mid_at + 1032 * n + 2 * width].bitcast(F32)

        node = mid(0)
        node_t = mid(1)
        x_res = mid(2)
        wh = mid(3, IT * HW).rearrange("p (t c) -> p t c", t=IT)
        v_new = second_arena[:, mid_at + 4 * 1032:mid_at + 6 * 1032].bitcast(F16).rearrange(
            "p (t k c) -> p t k c", t=IT, k=2)
        x_all = mask[:, NG - 1, :].bitcast(F32).rearrange("p (t c) -> p t c", t=NT)
        x_rest = mask[:, NG - 2, :].bitcast(F32).rearrange("p (t c) -> p t c", t=NT)
        v_all = first_arena[:, 0:NT * 2 * VW].bitcast(F16).rearrange("p (t k c) -> p t k c", t=NT, k=2)
        y_code = second_arena[:, 0:RING * GI].rearrange("p (s c) -> p s c", s=RING)
        n_pos = second_arena[:, RING * GI:2 * RING * GI].rearrange("p (s c) -> p s c", s=RING)
        n_neg = second_arena[:, 2 * RING * GI:3 * RING * GI].rearrange("p (s c) -> p s c", s=RING)
        f1_rows = second_arena[:, 3 * RING * GI:3 * RING * GI + 4 * GI].bitcast(F32)
        x1_back = sb("x1_back", [P, IT * F], F32)

        pos_sum = sb("pos_sum", [P, IT, VW], F32)
        both = pos_sum
        joined = sb("joined", [P, IT, HW], F32)
        h = sb("h", [P, IT * F], F32)
        h_exp = sb("h_exp", [P, IT * F], F32)

        ident = sb("ident", [P, P], F32)
        w0t_sb = sb("w0t_sb", [P, F], F32)
        w1_sb = sb("w1_sb", [P, F + 2], F32)
        w1t_sb = sb("w1t_sb", [P, F], F32)
        a_sb = sb("a_sb", [P, 2], F32)
        b_rows = sb("b_rows", [P, F], F32)
        wa_wide = sb("wa_wide", [P, P], F32)
        w_lim = sb("w_lim", [P, 4], F32)
        w_pow = sb("w_pow", [P, 1], F32)
        w_inv = sb("w_inv", [P, 1], F32)
        half = sb("half", [P, 1], F32)
        minus_half = sb("minus_half", [P, IT], F32)
        rdeg = sb("rdeg", [P, IT], F32)
        stats = sb("stats", [P, IT, 6], F32)
        moments = sb("moments", [P, IT, 2], F32)
        vare = sb("vare", [P, IT], F32)
        rstd = sb("rstd", [P, IT], F32)
        rden = sb("rden", [P, IT], F32)
        f_cols = sb("f_cols", [P, NT, 2], F32)
        thr = sb("thr", [P, NT], F32)
        weight = sb("weight", [P, NT, 2], F32)
        mant = sb("mant", [P, NT, 2], F32)
        scale = sb("scale", [P, NT, 2], F32)
        neg_scale = sb("neg_scale", [P, NT], F32)
        row_arg = sb("row_arg", [P, 2, NT], F32)
        row_fac = sb("row_fac", [P, 2, NT], F32)
        f1_out = sb("f1_out", [1, GI], F32)

        acc = ctx.enter_context(nc.psum_tensor("acc", [P, 8, 512], F32))
        sums = acc[:, 0:IT, :]
        agg_t_ps = acc[:, 4, :]
        lin_ps = acc[:, 5, :]
        x1_t_ps = acc[:, 6, :]
        wh_ps = acc[:, 6:8, 0:2 * (F + 2)].rearrange("p b (t c) -> p b t c", t=2)
        f1_ps = acc[:, 4, :]
        wa_ps = acc[:, 5, 0:2]

        held_vector, held_pool = sem("held_vector"), sem("held_pool")
        w_landed = sem("w_landed")
        x_landed = sem("x_landed")
        adj_landed = [sem(f"adj_landed{i}") for i in range(SLOTS)]
        xres_landed = sem("xres_landed")
        ident_ready = sem("ident_ready")
        consts_ready = sem("consts_ready")
        w_max_ready = sem("w_max_ready")
        w_all_ready = sem("w_all_ready")
        w_step = sem("w_step")
        wa_ready = sem("wa_ready")
        weights_ready = sem("weights_ready")
        x_hi_ready = sem("x_hi_ready")
        x_rest_ready = sem("x_rest_ready")
        x_mid_ready = sem("x_mid_ready")
        x_parts_ready = sem("x_parts_ready")
        a01_ready = sem("a01_ready")
        mask_ready = sem("mask_ready")
        chunk_used = sem("chunk_used")
        sums_ready = sem("sums_ready")
        sums_read = sem("sums_read")
        rdeg_ready = sem("rdeg_ready")
        agg_t_ready = sem("agg_t_ready")
        agg_t_copied = sem("agg_t_copied")
        lin_ready = sem("lin_ready")
        xb_ready = sem("xb_ready")
        y_ready = sem("y_ready")
        stats_ready = sem("stats_ready")
        moments_ready = sem("moments_ready")
        pool_step = sem("pool_step")
        rstd_ready = sem("rstd_ready")
        x1_ready = sem("x1_ready")
        x1_stored = sem("x1_stored")
        x1_t_ready = sem("x1_t_ready")
        x1_t_copied = sem("x1_t_copied")
        wh_ready = sem("wh_ready")
        f_copied = sem("f_copied")
        wh_copied = sem("wh_copied")
        f1_copied = sem("f1_copied")
        f1_stored = sem("f1_stored")
        weight_ready = sem("weight_ready")
        mant_ready = sem("mant_ready")
        v_hi_ready = sem("v_hi_ready")
        v_lo_ready = sem("v_lo_ready")
        v_stored = sem("v_stored")
        v_landed = sem("v_landed")
        f1_landed = [sem("f1_landed_even"), sem("f1_landed_odd")]
        row_arg_ready = sem("row_arg_ready")
        row_fac_ready = sem("row_fac_ready")
        code_ready = sem("code_ready")
        pos_ready = sem("pos_ready")
        neg_ready = sem("neg_ready")
        tile_used = sem("tile_used")
        acc_ready = sem("acc_ready")
        pos_read = sem("pos_read")
        acc_read = sem("acc_read")
        joined_ready = sem("joined_ready")
        rden_ready = sem("rden_ready")
        neg_part_ready = sem("neg_part_ready")
        exp_ready = sem("exp_ready")
        x1_back_landed = sem("x1_back_landed")
        res_ready = sem("res_ready")
        stats2_ready = sem("stats2_ready")
        moments2_ready = sem("moments2_ready")
        normed = sem("normed")
        out_landed = sem("out_landed")

        block = ctx.enter_context(nc.Block())


        @block.sync
        def _(sp):
            def load_chunks(g, first=False):
                for c in range(NC):
                    s = c % SLOTS
                    if not (first and c < SLOTS):
                        sp.wait_ge(a01_ready, g * NC + (c - SLOTS + 1))
                        sp.wait_ge(mask_ready, g * NC + (c - SLOTS + 1))
                    sp.dma_start(adj_in[:, s, :],
                                 adj_tiles[bass.ds(g, 1), :, c * CJ * GI:(c + 1) * CJ * GI].rearrange(
                                     "g p n -> (g p) n")).then_inc(adj_landed[s], 16)

            QX = NT // 4
            sp.dma_start(x_all[:, 0:QX, :], x_tiles[:, 0:QX, :]).then_inc(x_landed, 16)
            for c in range(SLOTS):
                sp.dma_start(adj_in[:, c, :], adj_tiles[0, :, c * CJ * GI:(c + 1) * CJ * GI]).then_inc(
                    adj_landed[c], 16)
            for c in range(SLOTS, NC):
                sp.wait_ge(a01_ready, c - SLOTS + 1)
                sp.wait_ge(mask_ready, c - SLOTS + 1)
                sp.dma_start(adj_in[:, c % SLOTS, :], adj_tiles[0, :, c * CJ * GI:(c + 1) * CJ * GI]).then_inc(
                    adj_landed[c % SLOTS], 16)
            with sp.Fori(1, NG) as g:
                load_chunks(g)

            sp.wait_ge(chunk_used, NG * NC)
            sp.wait_ge(a01_ready, NG * NC)
            sp.wait_ge(mask_ready, NG * NC)
            for g in range(NG):
                sp.wait_ge(v_stored, 16 * (g + 1))
                if g == NG - 1:
                    sp.wait_ge(x1_stored, 16 * NG)
                    sp.wait_ge(f1_stored, 16 * NG)
                    for k in range(2):
                        sp.dma_start(f1_rows[:, k * GI:(k + 1) * GI],
                                     f1_dram[k].to_broadcast([P, GI])).then_inc(f1_landed[k], 16)
                sp.dma_start(v_all[:, g * IT:(g + 1) * IT, :, :].rearrange("p t k c -> p (t k c)"),
                             v_dram[g]).then_inc(v_landed, 16)
            with sp.Fori(0, NG // 2 - 1) as k:
                for odd in range(2):
                    sp.wait_ge(code_ready, (k * 2 + (odd + 1)) * NT)
                    sp.dma_start(f1_rows[:, odd * GI:(odd + 1) * GI],
                                 f1_dram[bass.ds(k * 2 + (2 + odd), 1)].rearrange("g a n -> (g a) n")
                                 .to_broadcast([P, GI])).then_inc(f1_landed[odd], 16)

        @block.gpsimd
        def _(pool):
            def alone():
                pool.sem_inc(held_pool, 1)

            nc.gpsimd.memset(ident[:], 1.0).then_inc(ident_ready, 1)
            pool.wait_ge(ident_ready, 1)
            nc.gpsimd.affine_select(out=ident[:], in_=ident[:], compare_op=ALU.is_equal, fill=0.0, base=0,
                                    pattern=[[-1, P]], channel_multiplier=1).then_inc(ident_ready, 1)
            nc.gpsimd.memset(minus_half[:], -0.5).then_inc(consts_ready, 1)
            nc.gpsimd.memset(wh[:, :, F:HW], 1.0).then_inc(consts_ready, 1)
            for k in range(NG):
                t = slice(k * IT, (k + 1) * IT)
                pool.wait_ge(x_hi_ready, k + 1)
                nc.gpsimd.tensor_tensor(x_rest[:, t, :], x_all[:, t, :], xparts[:, t, 0:F],
                                        ALU.subtract).then_inc(x_rest_ready, 1)
                pool.wait_ge(x_mid_ready, k + 1)
                nc.gpsimd.tensor_tensor(xparts[:, t, 2 * F:3 * F], x_rest[:, t, :], xparts[:, t, F:2 * F],
                                        ALU.subtract).then_inc(x_parts_ready, 1)

            pool.wait_ge(w_max_ready, 1)
            nc.gpsimd.partition_all_reduce(w_lim[:, 3:4], w_lim[:, 2:3], P, bass.bass_isa.ReduceOp.max).then_inc(
                w_all_ready, 1)

            def rsqrt(n_moments, done, step):
                pool.wait_ge(n_moments[0], n_moments[1])
                alone()
                nc.gpsimd.tensor_scalar(vare[:], moments[:, :, 1], EPS, 0.0, ALU.add, ALU.add).then_inc(pool_step, 1)
                pool.wait_ge(pool_step, step)
                nc.gpsimd.tensor_tensor(rstd[:], vare[:], minus_half[:], ALU.pow).then_inc(done, 1)

            def first_layer_rows(g):
                pool.dma_start(x_res, x_tiles[:, bass.ds(g * IT, IT), :].rearrange("p t c -> p (t c)")).then_inc(
                    xres_landed, 16)
                pool.wait_ge(xres_landed, g * 16 + 16)
                for t in range(IT):
                    last = nc.gpsimd.tensor_tensor(x_res[:, t * F:(t + 1) * F], x_res[:, t * F:(t + 1) * F],
                                                   b_rows[:], ALU.add)
                last.then_inc(xb_ready, 1)
                rsqrt((moments_ready, g * IT + IT), rstd_ready, g + 1)
                pool.wait_ge(x1_ready, g * IT + IT)
                pool.dma_start(x1_dram[bass.ds(g, 1)].rearrange("g p n -> (g p) n"), node).then_inc(x1_stored, 16)
                pool.wait_ge(f1_copied, g + 1)
                pool.dma_start(f1_dram[bass.ds(g, 1)].rearrange("g a n -> (g a) n"), f1_out[:]).then_inc(
                    f1_stored, 16)
                pool.wait_ge(v_lo_ready, g * 2 * IT + 2 * IT)
                pool.dma_start(v_dram[bass.ds(g, 1)].rearrange("g p n -> (g p) n"),
                               v_new.rearrange("p t k c -> p (t k c)")).then_inc(v_stored, 16)

            pool.wait_ge(w_landed, 16 * 5)
            with pool.Fori(0, NG) as g:
                first_layer_rows(g)

            with pool.Fori(0, NG) as g:
                pool.wait_ge(v_stored, 16 * NG)
                pool.wait_ge(x1_stored, 16 * NG)
                pool.dma_start(x1_back[:], x1_dram[bass.ds(g, 1)].rearrange("g p n -> (g p) n")).then_inc(
                    x1_back_landed, 16)
                base = g * 5 + NG
                pool.wait_ge(acc_read, g * IT + IT)
                nc.gpsimd.tensor_tensor(joined[:], both[:, :, 0:HW], both[:, :, HW:VW], ALU.add).then_inc(
                    joined_ready, 1)
                pool.wait_ge(rden_ready, g + 1)
                alone()
                for t in range(IT):
                    last = nc.gpsimd.tensor_scalar(h[:, t * F:(t + 1) * F], joined[:, t, 0:F], rden[:, t:t + 1],
                                                   w_pow[:], ALU.mult, ALU.mult)
                last.then_inc(pool_step, 1)
                pool.wait_ge(pool_step, base + 1)
                alone()
                nc.gpsimd.tensor_scalar(h_exp[:], h[:], 0.0, 0.0, ALU.min, ALU.add).then_inc(neg_part_ready, 1)
                nc.gpsimd.tensor_scalar(h[:], h[:], 0.0, -1.0, ALU.max, ALU.add).then_inc(pool_step, 1)
                pool.wait_ge(pool_step, base + 2)
                pool.wait_ge(x1_back_landed, g * 16 + 16)
                nc.gpsimd.tensor_tensor(h[:], h[:], x1_back[:], ALU.add).then_inc(pool_step, 1)
                pool.wait_ge(pool_step, base + 3)
                pool.wait_ge(exp_ready, g + 1)
                nc.gpsimd.tensor_tensor(h[:], h[:], h_exp[:], ALU.add).then_inc(res_ready, 1)
                pool.wait_ge(moments2_ready, g * IT + IT)
                alone()
                nc.gpsimd.tensor_scalar(vare[:], moments[:, :, 1], EPS, 0.0, ALU.add, ALU.add).then_inc(pool_step, 1)
                pool.wait_ge(pool_step, base + 4)
                nc.gpsimd.tensor_tensor(rstd[:], vare[:], minus_half[:], ALU.pow).then_inc(pool_step, 1)
                pool.wait_ge(pool_step, base + 5)
                alone()
                for t in range(IT):
                    last = nc.gpsimd.tensor_scalar(h[:, t * F:(t + 1) * F], h[:, t * F:(t + 1) * F],
                                                   moments[:, t, 0:1], rstd[:, t:t + 1], ALU.subtract, ALU.mult)
                last.then_inc(normed, 1)
                pool.wait_ge(normed, g + 1)
                pool.dma_start(out_tiles[:, bass.ds(g * IT, IT), :].rearrange("p t c -> p (t c)"), h[:]).then_inc(
                    out_landed, 16)
                pool.wait_ge(out_landed, g * 16 + 16)

        @block.scalar
        def _(act):
            act.dma_start(w1_sb[:, 0:F], w1).then_inc(w_landed, 16)
            act.dma_start(w1t_sb[:], w1t).then_inc(w_landed, 16)
            act.dma_start(w0t_sb[:], w0t).then_inc(w_landed, 16)
            act.dma_start(a_sb[:], a_cols).then_inc(w_landed, 16)
            act.dma_start(b_rows[:], b0.to_broadcast([P, F])).then_inc(w_landed, 16)
            QX = NT // 4
            for q in range(1, 4):
                act.dma_start(x_all[:, q * QX:(q + 1) * QX, :], x_tiles[:, q * QX:(q + 1) * QX, :]).then_inc(
                    x_landed, 16)

            def keep_mask(g, c, lap):
                act.wait_ge(adj_landed[c % SLOTS], lap)
                nc.scalar.activation(mask[:, bass.ds(g, 1), c * CJ * GI:(c + 1) * CJ * GI].rearrange(
                    "p g n -> p (g n)"), adj_in[:, c % SLOTS, :], ACT.Sign, bias=half[:], scale=1.0).then_inc(
                        mask_ready, 1)

            def weights_of_nodes(g):
                act.wait_ge(f_copied, g + 1)
                nc.scalar.activation(weight[:, bass.ds(g * IT, IT), 0:1], f_cols[:, bass.ds(g * IT, IT), 1:2],
                                     ACT.Exp)
                nc.scalar.activation(weight[:, bass.ds(g * IT, IT), 1:2], f_cols[:, bass.ds(g * IT, IT), 1:2],
                                     ACT.Exp, scale=ALPHA).then_inc(weight_ready, 1)
                act.wait_ge(mant_ready, g + 1)
                act.wait_ge(wh_copied, g + 1)

            def high_parts(g, first=False):
                if not first:
                    act.wait_ge(v_stored, g * 16)
                for t in range(IT):
                    for k in range(2):
                        nc.scalar.activation(v_new[:, t, k, 0:HW], wh[:, t, :], ACT.Copy,
                                             scale=mant[:, bass.ds(g * IT + t, 1), k:k + 1].rearrange(
                                                 "p t k -> p (t k)")).then_inc(v_hi_ready, 1)

            act.wait_ge(consts_ready, 3)
            for c in range(NC):
                keep_mask(0, c, 16 * (c // SLOTS + 1))
            laps = NC // SLOTS

            def group(g, first=False):
                for c in range(NC):
                    keep_mask(g, c, g * 16 * laps + 16 * (c // SLOTS + 1))
                weights_of_nodes(g - 1)
                high_parts(g - 1, first)

            act.wait_ge(x_parts_ready, NG)
            group(1, True)
            with act.Fori(2, NG) as g:
                group(g)
            weights_of_nodes(NG - 1)
            high_parts(NG - 1)

            act.wait_ge(row_arg_ready, 1)
            nc.scalar.activation(row_fac[:], row_arg[:], ACT.Exp).then_inc(row_fac_ready, 1)
            act.wait_ge(row_fac_ready, 1)

            def positive_tile(g, jt, s):
                act.wait_ge(code_ready, g * NT + (jt + 1))
                if not (isinstance(g, int) and g == 0 and isinstance(jt, int)):
                    act.wait_ge(tile_used, g * NT + (jt - (RING - 1)))
                nc.scalar.activation(n_pos[:, s, :], y_code[:, s, :], ACT.Relu,
                                     bias=neg_scale[:, bass.ds(jt, 1)],
                                     scale=scale[:, bass.ds(jt, 1), 0:1].rearrange("p t k -> p (t k)")).then_inc(
                                         pos_ready, 1)

            def read_positive(g, first=False):
                for t in range(IT):
                    if t < IT - 1:
                        act.wait_ge(acc_ready, g * (IT - 1) + (t + 1))
                    else:
                        act.wait_ge(tile_used, g * NT + NT)
                    if not first:
                        act.wait_ge(joined_ready, g)
                    nc.scalar.activation(pos_sum[:, t, :], acc[:, 2 * t, 0:VW], ACT.Copy,
                                         scale=row_fac[:, 0, bass.ds(g * IT + t, 1)]).then_inc(pos_read, 1)

            def elu_exp(g):
                act.wait_ge(neg_part_ready, g + 1)
                nc.scalar.activation(h_exp[:], h_exp[:], ACT.Exp).then_inc(exp_ready, 1)

            def quads(g, q0, q1):
                with act.Fori(q0, q1) as q:
                    for s in range(RING):
                        positive_tile(g, q * RING + s, s)

            def group1(g, tail=True, first=False):
                for s in range(2):
                    positive_tile(g, s, s)
                if tail:
                    read_positive(g - 1, first)
                for s in range(2, RING):
                    positive_tile(g, s, s)
                quads(g, 1, 4)
                if tail:
                    elu_exp(g - 1)
                quads(g, 4, NT // RING)

            group1(0, tail=False)
            group1(1, first=True)
            with act.Fori(2, NG) as g:
                group1(g)
            read_positive(NG - 1)
            elu_exp(NG - 1)

        @block.tensor
        def _(pe):
            pe.wait_ge(w_landed, 16 * 5)
            nc.tensor.matmul(wa_ps, w1t_sb[:], a_sb[:], start=True, stop=True).then_inc(wa_ready, 1)

            def chunk(g, c):
                pe.wait_ge(a01_ready, g * NC + (c + 1))
                if isinstance(g, int) and c % 2 == 0:
                    pe.wait_ge(x_parts_ready, c // 2 + 1)
                for j in range(CJ):
                    jt = c * CJ + j
                    for t in range(IT):
                        if jt == 0 and not (isinstance(g, int)):
                            pe.wait_ge(sums_read, g * IT + (t - IT + 1))
                        mm = nc.tensor.matmul(sums[:, t, 0:XW],
                                              a01[:, c % SLOTS, j * GI + t * P:j * GI + (t + 1) * P],
                                              xparts[:, jt, :], start=(jt == 0), stop=(jt == NT - 1))
                        if j == CJ - 1 and t == IT - 1:
                            mm.then_inc(chunk_used, 1)
                        elif jt == NT - 1:
                            mm.then_inc(sums_ready, 1)

            def turn_sums(g):
                pe.wait_ge(sums_read, g * IT + IT)
                for t in range(IT):
                    mm = nc.tensor.transpose(agg_t_ps[:, t * P:(t + 1) * P], node[:, t * F:(t + 1) * F], ident[:])
                mm.then_inc(agg_t_ready, 1)

            def linear(g):
                pe.wait_ge(agg_t_copied, g + 1)
                for t in range(IT):
                    mm = nc.tensor.matmul(lin_ps[:, t * F:(t + 1) * F], node_t[:, t * P:(t + 1) * P], w0t_sb[:],
                                          start=True, stop=True)
                mm.then_inc(lin_ready, 1)

            def turn_x1(g):
                pe.wait_ge(x1_ready, g * IT + IT)
                for t in range(IT):
                    mm = nc.tensor.transpose(x1_t_ps[:, t * P:(t + 1) * P], node[:, t * F:(t + 1) * F], ident[:])
                mm.then_inc(x1_t_ready, 1)

            def project(g):
                pe.wait_ge(x1_t_copied, g + 1)
                for t in range(IT):
                    nc.tensor.matmul(wh_ps[:, t // 2, t % 2, :], node_t[:, t * P:(t + 1) * P], w1_sb[:],
                                     start=True, stop=True)
                nc.tensor.matmul(f1_ps, wa_wide[:], node_t, start=True, stop=True).then_inc(wh_ready, 1)

            pe.wait_ge(ident_ready, 2)
            def run_chunks(g, c0, c1):
                for c in range(c0, c1):
                    chunk(g, c)

            def group(g):
                run_chunks(g, 0, 4)
                turn_sums(g - 1)
                run_chunks(g, 4, 7)
                linear(g - 1)
                run_chunks(g, 7, 11)
                turn_x1(g - 1)
                run_chunks(g, 11, 14)
                project(g - 1)
                run_chunks(g, 14, NC)

            run_chunks(0, 0, NC)
            pe.wait_ge(weights_ready, 1)
            with pe.Fori(1, NG) as g:
                group(g)
            turn_sums(NG - 1)
            linear(NG - 1)
            turn_x1(NG - 1)
            project(NG - 1)

            def tile(g, jt, s, start, stop):
                pe.wait_ge(pos_ready, g * NT + (jt + 1))
                pe.wait_ge(neg_ready, g * NT + (jt + 1))
                for t in range(IT):
                    if start and not isinstance(g, int):
                        pe.wait_ge(acc_read, g * IT + (t + 1 - IT))
                    for k, tiles in enumerate((n_pos, n_neg)):
                        mm = nc.tensor.matmul(acc[:, 2 * t + k, 0:VW], tiles[:, s, t * P:(t + 1) * P],
                                              v_all[:, bass.ds(jt, 1), k, :].rearrange("p t c -> p (t c)"),
                                              start=start, stop=stop)
                    if t == IT - 1:
                        mm.then_inc(tile_used, 1)
                    elif stop:
                        mm.then_inc(acc_ready, 1)

            def group1(g):
                if isinstance(g, int):
                    pe.wait_ge(v_landed, 16 * NG)
                for s in range(RING):
                    tile(g, s, s, s == 0, False)
                with pe.Fori(1, NT // RING - 1) as q:
                    for s in range(RING):
                        tile(g, q * RING + s, s, False, False)
                for s in range(RING):
                    tile(g, NT - RING + s, s, False, s == RING - 1)

            pe.wait_ge(wh_copied, NG)
            pe.wait_ge(f1_copied, NG)
            group1(0)
            with pe.Fori(1, NG) as g:
                group1(g)

        @block.vector
        def _(dve):
            def alone():
                dve.sem_inc(held_vector, 1)

            nc.vector.memset(half[:], -0.5).then_inc(consts_ready, 1)
            nc.vector.memset(xparts[:, :, 3 * F:XW], 1.0).then_inc(w_step, 1)
            for k in range(NG):
                t = slice(k * IT, (k + 1) * IT)
                dve.wait_ge(x_landed, 64)
                nc.vector.tensor_copy(xparts[:, t, 0:F], x_all[:, t, :]).then_inc(x_hi_ready, 1)

            def binarise(g, c, lap):
                s = c % SLOTS
                dve.wait_ge(adj_landed[s], lap)
                if not (isinstance(g, int) and g == 0 and c < SLOTS):
                    dve.wait_ge(chunk_used, g * NC + (c - SLOTS + 1))
                nc.vector.tensor_scalar(a01[:, s, :], adj_in[:, s, :], 1.0, None, ALU.is_equal).then_inc(a01_ready, 1)

            def middle_part(k):
                t = slice(k * IT, (k + 1) * IT)
                dve.wait_ge(x_rest_ready, k + 1)
                nc.vector.tensor_copy(xparts[:, t, F:2 * F], x_rest[:, t, :]).then_inc(x_mid_ready, 1)

            for c in range(NC):
                binarise(0, c, 16 * (c // SLOTS + 1))
                if c % 2 == 0:
                    middle_part(c // 2)

            dve.wait_ge(w_landed, 16 * 5)
            nc.vector.tensor_reduce(w_lim[:, 0:1], w1_sb[:, 0:F], AX.X, ALU.max).then_inc(w_step, 1)
            nc.vector.tensor_reduce(w_lim[:, 1:2], w1_sb[:, 0:F], AX.X, ALU.min).then_inc(w_step, 1)
            dve.wait_ge(w_step, 3)
            nc.vector.scalar_tensor_tensor(w_lim[:, 2:3], w_lim[:, 1:2], -1.0, w_lim[:, 0:1], ALU.mult,
                                           ALU.max).then_inc(w_max_ready, 1)
            dve.wait_ge(w_all_ready, 1)
            nc.vector.tensor_scalar(w_lim[:, 2:3], w_lim[:, 3:4], 1e-30, 1e37, ALU.max, ALU.min).then_inc(w_step, 1)
            dve.wait_ge(w_step, 4)
            nc.vector.tensor_scalar(w_pow[:].bitcast(I32), w_lim[:, 2:3].bitcast(I32), EXP_BITS, None,
                                    ALU.bitwise_and).then_inc(w_step, 1)
            dve.wait_ge(w_step, 5)
            nc.vector.reciprocal(w_inv[:], w_pow[:]).then_inc(w_step, 1)
            dve.wait_ge(w_step, 6)
            nc.vector.tensor_scalar(w1_sb[:, 0:F], w1_sb[:, 0:F], w_inv[:], None, ALU.mult).then_inc(w_step, 1)
            dve.wait_ge(wa_ready, 1)
            nc.vector.tensor_copy(w1_sb[:, F:F + 2], wa_ps).then_inc(w_step, 1)
            dve.wait_ge(w_step, 8)
            nc.vector.tensor_copy(wa_wide[:], w1_sb[:, F:F + 1].to_broadcast([P, P])).then_inc(weights_ready, 1)

            laps = NC // SLOTS

            def read_sums(g, first=False):
                if not first:
                    dve.wait_ge(x1_stored, g * 16)
                for t in range(IT):
                    if t < IT - 1:
                        dve.wait_ge(sums_ready, g * (IT - 1) + (t + 1))
                    else:
                        dve.wait_ge(chunk_used, g * NC + NC)
                    nc.vector.reciprocal(rdeg[:, t:t + 1], sums[:, t, 3 * F:XW])
                    nc.vector.tensor_reduce(node[:, t * F:(t + 1) * F],
                                            sums[:, t, 0:3 * F].rearrange("p (k f) -> p f k", k=3),
                                            AX.X, ALU.add).then_inc(sums_read, 1)

            def copy_sums_t(g):
                dve.wait_ge(agg_t_ready, g + 1)
                nc.vector.tensor_copy(node_t, agg_t_ps).then_inc(agg_t_copied, 1)

            def residual(g):
                dve.wait_ge(lin_ready, g + 1)
                dve.wait_ge(xb_ready, g + 1)
                for t in range(IT):
                    f = slice(t * F, (t + 1) * F)
                    nc.vector.scalar_tensor_tensor(node[:, f], lin_ps[:, f], rdeg[:, t:t + 1], x_res[:, f],
                                                   ALU.mult, ALU.add).then_inc(y_ready, 1)
                for t in range(IT):
                    dve.wait_ge(y_ready, g * IT + (t + 1))
                    nc.vector.bn_stats(stats[:, t, :], node[:, t * F:(t + 1) * F]).then_inc(stats_ready, 1)
                for t in range(IT):
                    dve.wait_ge(stats_ready, g * IT + (t + 1))
                    alone()
                    nc.vector.bn_aggr(moments[:, t, :], stats[:, t, :]).then_inc(moments_ready, 1)

            def normalise(g):
                dve.wait_ge(rstd_ready, g + 1)
                for t in range(IT):
                    f = slice(t * F, (t + 1) * F)
                    nc.vector.tensor_scalar(node[:, f], node[:, f], moments[:, t, 0:1], rstd[:, t:t + 1],
                                            ALU.subtract, ALU.mult).then_inc(x1_ready, 1)

            def copy_x1_t(g):
                dve.wait_ge(x1_t_ready, g + 1)
                nc.vector.tensor_copy(node_t, x1_t_ps).then_inc(x1_t_copied, 1)

            def take_projections(g, first=False):
                dve.wait_ge(wh_ready, g + 1)
                fc = f_cols[:, bass.ds(g * IT, IT), :]
                nc.vector.tensor_copy(fc.rearrange("p (b t) c -> p b t c", b=2), wh_ps[:, :, :, F:F + 2]).then_inc(
                    f_copied, 1)
                nc.vector.tensor_copy(wh[:, :, 0:F].rearrange("p (b t) c -> p b t c", b=2),
                                      wh_ps[:, :, :, 0:F]).then_inc(wh_copied, 1)
                if not first:
                    dve.wait_ge(f1_stored, g * 16)
                nc.vector.tensor_copy(f1_out[:], f1_ps[0:1, :]).then_inc(f1_copied, 1)
                dve.wait_ge(f_copied, g + 1)
                nc.vector.tensor_scalar(thr[:, bass.ds(g * IT, IT)],
                                        f_cols[:, bass.ds(g * IT, IT), 1:2].rearrange("p t k -> p (t k)"),
                                        -1.0, None, ALU.mult)
                dve.wait_ge(weight_ready, g + 1)
                wt = weight[:, bass.ds(g * IT, IT), :].bitcast(I32)
                nc.vector.tensor_scalar(scale[:, bass.ds(g * IT, IT), :].bitcast(I32), wt, EXP_BITS, None,
                                        ALU.bitwise_and)
                nc.vector.tensor_scalar(mant[:, bass.ds(g * IT, IT), :].bitcast(I32), wt, MAN_BITS, BITS_64,
                                        ALU.bitwise_and, ALU.bitwise_or).then_inc(mant_ready, 1)

            def low_parts(g):
                for t in range(IT):
                    for k in range(2):
                        dve.wait_ge(v_hi_ready, g * 2 * IT + (2 * t + k + 1))
                        nc.vector.scalar_tensor_tensor(
                            v_new[:, t, k, HW:VW], wh[:, t, :],
                            mant[:, bass.ds(g * IT + t, 1), k:k + 1].rearrange("p t k -> p (t k)"),
                            v_new[:, t, k, 0:HW], ALU.mult, ALU.subtract).then_inc(v_lo_ready, 1)

            def group(g, first=False):
                def run(c0, c1):
                    for c in range(c0, c1):
                        binarise(g, c, g * 16 * laps + 16 * (c // SLOTS + 1))
                run(0, 2)
                read_sums(g - 1, first)
                run(2, 6)
                copy_sums_t(g - 1)
                run(6, 9)
                residual(g - 1)
                run(9, 11)
                normalise(g - 1)
                run(11, 13)
                copy_x1_t(g - 1)
                run(13, NC)
                take_projections(g - 1, first)
                low_parts(g - 1)

            group(1, True)
            with dve.Fori(2, NG) as g:
                group(g)
            L = NG - 1
            read_sums(L)
            copy_sums_t(L)
            residual(L)
            normalise(L)
            copy_x1_t(L)
            take_projections(L)
            low_parts(L)

            nc.vector.tensor_scalar(row_arg[:, 0, :], f_cols[:, :, 0], 0.0, 1.0 - ALPHA, ALU.min, ALU.mult)
            nc.vector.tensor_scalar(row_arg[:, 1, :], f_cols[:, :, 0], 0.0, ALPHA - 1.0, ALU.max,
                                    ALU.mult).then_inc(row_arg_ready, 1)
            nc.vector.tensor_scalar(neg_scale[:], scale[:, :, 0], -1.0, None, ALU.mult).then_inc(w_step, 1)
            dve.wait_ge(w_step, 9)
            dve.wait_ge(row_arg_ready, 1)
            dve.wait_ge(v_stored, 16 * NG)

            def code_tile(g, odd, jt, s):
                if not (isinstance(g, int) and g == 0 and isinstance(jt, int)):
                    dve.wait_ge(pos_ready, g * NT + (jt - (RING - 1)))
                nc.vector.scalar_tensor_tensor(
                    y_code[:, s, :], f1_rows[:, odd * GI:(odd + 1) * GI], thr[:, bass.ds(jt, 1)],
                    mask[:, bass.ds(g, 1), bass.ds(jt * GI, GI)].rearrange("p g n -> p (g n)"),
                    ALU.is_ge, ALU.add).then_inc(code_ready, 1)

            def negative_tile(g, jt, s):
                if not (isinstance(g, int) and g == 0 and isinstance(jt, int)):
                    dve.wait_ge(tile_used, g * NT + (jt - (RING - 1)))
                dve.wait_ge(code_ready, g * NT + (jt + 1))
                nc.vector.tensor_scalar(n_neg[:, s, :], y_code[:, s, :], 1.0,
                                        scale[:, bass.ds(jt, 1), 1:2].rearrange("p t k -> p (t k)"),
                                        ALU.is_equal, ALU.mult).then_inc(neg_ready, 1)

            def read_both(g):
                for t in range(IT):
                    dve.wait_ge(pos_read, g * IT + (t + 1))
                    nc.vector.scalar_tensor_tensor(both[:, t, :], acc[:, 2 * t + 1, 0:VW],
                                                   row_fac[:, 1, bass.ds(g * IT + t, 1)], pos_sum[:, t, :],
                                                   ALU.mult, ALU.add).then_inc(acc_read, 1)

            def inverse_denominators(g):
                dve.wait_ge(joined_ready, g + 1)
                nc.vector.reciprocal(rden[:], joined[:, :, F]).then_inc(rden_ready, 1)

            def moments2(g):
                dve.wait_ge(res_ready, g + 1)
                for t in range(IT):
                    nc.vector.bn_stats(stats[:, t, :], h[:, t * F:(t + 1) * F]).then_inc(stats2_ready, 1)
                for t in range(IT):
                    dve.wait_ge(stats2_ready, g * IT + (t + 1))
                    alone()
                    nc.vector.bn_aggr(moments[:, t, :], stats[:, t, :]).then_inc(moments2_ready, 1)

            def run(g, odd, jts, slots):
                pending = None
                for jt, s in zip(jts, slots):
                    code_tile(g, odd, jt, s)
                    if pending:
                        negative_tile(g, *pending)
                    pending = (jt, s)
                negative_tile(g, *pending)

            def quads(g, odd, q0, q1):
                with dve.Fori(q0, q1) as q:
                    run(g, odd, [q * RING + s for s in range(RING)], range(RING))

            def group1(g, odd, tail=True):
                run(g, odd, range(2), range(2))
                if tail:
                    read_both(g - 1)
                run(g, odd, range(2, RING), range(2, RING))
                quads(g, odd, 1, 3)
                if tail:
                    inverse_denominators(g - 1)
                quads(g, odd, 3, 6)
                if tail:
                    moments2(g - 1)
                quads(g, odd, 6, NT // RING)

            dve.wait_ge(row_fac_ready, 1)
            dve.wait_ge(f1_landed[0], 16)
            group1(0, 0, tail=False)
            dve.wait_ge(f1_landed[1], 16)
            group1(1, 1)
            with dve.Fori(1, NG // 2) as k:
                for odd in range(2):
                    dve.wait_ge(f1_landed[odd], k * 16 + 16)
                    group1(k * 2 + odd, odd)
            read_both(NG - 1)
            inverse_denominators(NG - 1)
            moments2(NG - 1)


def kernel(x, adj, L0_gnn_W, L0_gnn_b, L1_gnn_W, L1_gnn_a):
    import numpy as np
    import concourse.bacc as bacc
    from concourse.bass_utils import run_bass_kernel_spmd

    adj_t = np.asarray(adj).T.reshape(NT, P, NG, GI).transpose(2, 1, 0, 3).reshape(NG, P, NT * GI)
    arrays = {
        "x_tiles": np.asarray(x).reshape(NT, P, F).transpose(1, 0, 2),
        "adj_tiles": adj_t,
        "w0t": np.asarray(L0_gnn_W).T,
        "b0": np.asarray(L0_gnn_b).reshape(1, F),
        "w1": np.asarray(L1_gnn_W),
        "w1t": np.asarray(L1_gnn_W).T,
        "a_cols": np.asarray(L1_gnn_a).reshape(2, F).T,
    }
    arrays = {k: np.ascontiguousarray(v) for k, v in arrays.items()}
    nc = bacc.Bacc("TRN2", target_bir_lowering=False, num_devices=1)
    args = [nc.dram_tensor(k, v.shape, mybir.dt.from_np(v.dtype), kind="ExternalInput").ap()
            for k, v in arrays.items()]
    out = nc.dram_tensor("out_tiles", (P, NT, F), F32, kind="ExternalOutput").ap()
    build(nc, *args, out)
    r = run_bass_kernel_spmd(nc, [arrays], core_ids=[0])
    got = r.results[0]["out_tiles"]
    return np.ascontiguousarray(got.transpose(1, 0, 2).reshape(N, F))
```

```python
from contextlib import ExitStack

import concourse.bass as bass
from concourse import mybir

ALU = mybir.AluOpType
ACT = mybir.ActivationFunctionType
AX = mybir.AxisListType
F32, BF16, F16, F8 = mybir.dt.float32, mybir.dt.bfloat16, mybir.dt.float16, mybir.dt.float8e5
I32, I8 = mybir.dt.int32, mybir.dt.int8

P = 128
N = 4096
F = 128
NT = N // P
GI = 512
NG = N // GI
IT = GI // P
CJ = 2
NC = NT // CJ
SLOTS = 4
LAPS = NC // SLOTS
XW = 3 * F + 1
HW = F + 1
VW = 2 * HW
RING = 8
GW = GI // 4
EPS = 1e-5
ALPHA = 0.2
EXP_BITS = 0x7F800000
F32_BIAS, F8_BIAS = 127, 15
F8_LOW, F8_HIGH = F32_BIAS - 14, F32_BIAS + 15
F1_LIMIT, F2_LIMIT = 40.0, 9.5
WIDE = 3e38
MANT_SHIFT = 2


def build(nc, x_tiles, adj_tiles, w0t, b0, w1, w1t, a_cols, out_tiles):
    ctx = ExitStack()
    with ctx:
        def sb(name, shape, dt):
            return ctx.enter_context(nc.sbuf_tensor(name, shape, dt))

        def sem(name):
            return ctx.enter_context(nc.semaphore(name))

        x1_dram = nc.dram_tensor("x1_scratch", [NG, P, IT * F], F32, kind="Internal").ap()
        f1_dram = nc.dram_tensor("f1_scratch", [NG, 1, GI], F32, kind="Internal").ap()
        v_dram = nc.dram_tensor("v_scratch", [NG - 1, P, IT * 2 * VW], F16, kind="Internal").ap()

        mask = sb("mask", [P, NG, NT * GW], I32)
        arena_a = sb("arena_a", [P, NT * XW + SLOTS * CJ * GI * 2], BF16)
        arena_b = sb("arena_b", [P, 3 * RING * GW], I32)
        arena_c = sb("arena_c", [P, 3096], F32)
        xparts = arena_a[:, 0:NT * XW].rearrange("p (t c) -> p t c", t=NT)
        adj_in = arena_a[:, NT * XW:].bitcast(I32).rearrange("p (s c) -> p s c", s=SLOTS)
        a01 = arena_b[:, 0:SLOTS * CJ * GI // 2].bitcast(BF16).rearrange("p (s c) -> p s c", s=SLOTS)
        node = arena_c[:, 0:512]
        node_t = arena_c[:, 512:1024]
        x_res = arena_c[:, 1024:1536]
        wh = arena_c[:, 1536:1536 + IT * HW].rearrange("p (t c) -> p t c", t=IT)
        v_new = arena_c[:, 2056:2056 + IT * VW].bitcast(F16).rearrange("p (t k c) -> p t k c", t=IT, k=2)
        x_all = mask[:, NG - 1, :].bitcast(F32).rearrange("p (t c) -> p t c", t=NT)
        x_rest = mask[:, NG - 2, :].bitcast(F32).rearrange("p (t c) -> p t c", t=NT)
        v_all = arena_a[:, 0:NT * 2 * VW].bitcast(F16).rearrange("p (t k c) -> p t k c", t=NT, k=2)
        neg_sum = arena_a[:, NT * 2 * VW:NT * 2 * VW + 2 * IT * VW].bitcast(F32).rearrange(
            "p (t c) -> p t c", t=IT)
        sign = arena_b[:, 0:RING * GW].rearrange("p (s c) -> p s c", s=RING)
        n_pos = arena_b[:, RING * GW:2 * RING * GW].rearrange("p (s c) -> p s c", s=RING)
        n_neg = arena_b[:, 2 * RING * GW:3 * RING * GW].rearrange("p (s c) -> p s c", s=RING)
        x1_back = arena_c[:, 0:512]
        pos_sum = arena_c[:, 512:512 + IT * VW].rearrange("p (t c) -> p t c", t=IT)
        joined = arena_c[:, 1544:1544 + IT * HW].rearrange("p (t c) -> p t c", t=IT)
        h_exp = arena_c[:, 1544:1544 + 512]
        h = arena_c[:, 2060:2572]
        h_min = arena_c[:, 2572:3084]

        wide_wh = arena_a[:, 0:NT * HW * 2].bitcast(F32).rearrange("p (t c) -> p t c", t=NT)
        wide_total = arena_a[:, NT * HW * 2:(NT + IT) * HW * 2].bitcast(F32).rearrange("p (t c) -> p t c", t=IT)
        wide_b = arena_b.rearrange("p (k c) -> p k c", k=6).bitcast(F32)
        wide_sum, wide_prob, wide_is, wide_cand, wide_best, wide_max = (wide_b[:, k, :] for k in range(6))

        not_pos = sb("not_pos", [P, 2, GW], I32)
        f1_rows = sb("f1_rows", [P, 2 * GI], F32)
        ident = sb("ident", [P, P], F32)
        w0t_sb = sb("w0t_sb", [P, F], F32)
        w1_sb = sb("w1_sb", [P, F + 2], F32)
        w1t_sb = sb("w1t_sb", [P, F], F32)
        a_sb = sb("a_sb", [P, 2], F32)
        b_rows = sb("b_rows", [P, F], F32)
        wa_wide = sb("wa_wide", [P, P], F32)
        w_lim = sb("w_lim", [P, 4], F32)
        w_pow = sb("w_pow", [P, 1], F32)
        w_inv = sb("w_inv", [P, 1], F32)
        half = sb("half", [P, 1], F32)
        minus_half = sb("minus_half", [P, IT], F32)
        eps_cols = sb("eps_cols", [P, IT], F32)
        rdeg = sb("rdeg", [P, IT], F32)
        stats = sb("stats", [P, IT, 6], F32)
        moments = sb("moments", [P, IT, 2], F32)
        vare = sb("vare", [P, IT], F32)
        rstd = sb("rstd", [P, IT], F32)
        rden = sb("rden", [P, IT], F32)
        f_cols = sb("f_cols", [P, NT, 2], F32)
        thr = sb("thr", [P, NT], F32)
        weight = sb("weight", [P, IT, 2], F32)
        w_exp = sb("w_exp", [P, 2, IT, 2], I32)
        w_unit = sb("w_unit", [P, 2, IT, 2], I32)
        mant = sb("mant", [P, IT, 2], F32)
        power = sb("power", [P, NT * 2, 4], I8)
        row_arg = sb("row_arg", [P, 2, NT], F32)
        row_fac = sb("row_fac", [P, 2, NT], F32)
        f1_out = sb("f1_out", [1, GI], F32)
        f_lim = sb("f_lim", [P, 8], F32)
        is_wide = sb("is_wide", [P, 1], I32)

        acc = ctx.enter_context(nc.psum_tensor("acc", [P, 8, 512], F32))
        sums = acc[:, 0:IT, :]
        agg_t_ps = acc[:, 4, :]
        lin_ps = acc[:, 5, :]
        x1_t_ps = acc[:, 6, :]
        wh_ps = acc[:, 6:8, 0:2 * (F + 2)].rearrange("p b (t c) -> p b t c", t=2)
        f1_ps = acc[:, 4, :]
        wa_ps = acc[:, 5, 0:2]

        wide_turned_ps = acc[:, 0, :]
        wide_wh_ps = acc[:, 1, :]
        wide_part = acc[:, 4:8, 0:HW]

        held_vector, held_pool, held_pe, held_sp = (sem("held_vector"), sem("held_pool"), sem("held_pe"),
                                                    sem("held_sp"))
        w_landed = sem("w_landed")
        XQ = 4
        x_landed = [sem(f"x_landed{i}") for i in range(XQ)]
        adj_landed = [sem(f"adj_landed{i}") for i in range(SLOTS)]
        xres_landed = sem("xres_landed")
        ident_ready = sem("ident_ready")
        consts_ready = sem("consts_ready")
        w_max_ready = sem("w_max_ready")
        w_all_ready = sem("w_all_ready")
        w_step = sem("w_step")
        wa_ready = sem("wa_ready")
        weights_ready = sem("weights_ready")
        x_hi_ready = sem("x_hi_ready")
        x_rest_ready = sem("x_rest_ready")
        x_mid_ready = sem("x_mid_ready")
        x_parts_ready = sem("x_parts_ready")
        a01_ready = sem("a01_ready")
        mask_ready = sem("mask_ready")
        chunk_used = sem("chunk_used")
        sums_ready = sem("sums_ready")
        sums_read = sem("sums_read")
        agg_t_ready = sem("agg_t_ready")
        agg_t_copied = sem("agg_t_copied")
        lin_ready = sem("lin_ready")
        xb_ready = sem("xb_ready")
        y_ready = sem("y_ready")
        stats_ready = sem("stats_ready")
        moments_ready = sem("moments_ready")
        pool_step = sem("pool_step")
        rstd_ready = sem("rstd_ready")
        x1_ready = sem("x1_ready")
        x1_stored = sem("x1_stored")
        x1_t_ready = sem("x1_t_ready")
        x1_t_copied = sem("x1_t_copied")
        wh_ready = sem("wh_ready")
        f1_ready = sem("f1_ready")
        f_copied = sem("f_copied")
        wh_copied = sem("wh_copied")
        f1_copied = sem("f1_copied")
        f1_stored = sem("f1_stored")
        weight_ready = sem("weight_ready")
        w_bits = sem("w_bits")
        mant_ready = sem("mant_ready")
        v_hi_ready = sem("v_hi_ready")
        v_lo_ready = sem("v_lo_ready")
        v_stored = sem("v_stored")
        v_landed = sem("v_landed")
        f1_landed = [sem("f1_landed_even"), sem("f1_landed_odd")]
        row_arg_ready = sem("row_arg_ready")
        row_fac_ready = sem("row_fac_ready")
        sign_ready = sem("sign_ready")
        pos_ready = sem("pos_ready")
        not_pos_ready = sem("not_pos_ready")
        neg_ready = sem("neg_ready")
        tile_used = sem("tile_used")
        acc_ready = sem("acc_ready")
        pos_read = sem("pos_read")
        neg_read = sem("neg_read")
        row_step, last_step = sem("row_step"), sem("last_step")
        joined_ready = sem("joined_ready")
        inv_ready = sem("inv_ready")
        rden_ready = sem("rden_ready")
        h_ready = sem("h_ready")
        min_ready = sem("min_ready")
        exp_ready = sem("exp_ready")
        elu_ready = sem("elu_ready")
        x1_back_landed = sem("x1_back_landed")
        res_ready = sem("res_ready")
        stats2_ready = sem("stats2_ready")
        moments2_ready = sem("moments2_ready")
        rstd2_ready = sem("rstd2_ready")
        normed = sem("normed")
        out_landed = sem("out_landed")
        lim_step = sem("lim_step")
        lim_ready = sem("lim_ready")
        lim_all_ready = sem("lim_all_ready")
        wide_known = sem("wide_known")
        wide_x1_landed = sem("wide_x1_landed")
        wide_turned = sem("wide_turned")
        wide_turned_copied = sem("wide_turned_copied")
        wide_wh_made = sem("wide_wh_made")
        wide_wh_copied = sem("wide_wh_copied")
        wide_rows_landed = sem("wide_rows_landed")
        wide_step = sem("wide_step")
        wide_best_ready = sem("wide_best_ready")
        wide_max_ready = sem("wide_max_ready")
        wide_arg_ready = sem("wide_arg_ready")
        wide_exp_ready = sem("wide_exp_ready")
        wide_prob_ready = sem("wide_prob_ready")
        wide_part_ready = sem("wide_part_ready")
        wide_part_added = sem("wide_part_added")
        wide_min_ready = sem("wide_min_ready")
        wide_elu_ready = sem("wide_elu_ready")
        wide_moments_ready = sem("wide_moments_ready")
        wide_pool_step = sem("wide_pool_step")
        wide_rstd_ready = sem("wide_rstd_ready")
        wide_normed = sem("wide_normed")
        wide_out_landed = sem("wide_out_landed")

        block = ctx.enter_context(nc.Block())
        LAST = NG - 1

        def sums_done(eng, g, t):
            if t < IT - 1:
                eng.wait_ge(sums_ready, g * (IT - 1) + (t + 1))
            else:
                eng.wait_ge(chunk_used, g * NC + NC)

        def acc_done(eng, g, t):
            if t < IT - 1:
                eng.wait_ge(acc_ready, g * (IT - 1) + (t + 1))
            else:
                eng.wait_ge(tile_used, g * NT + NT)

        def rows(t):
            return slice(t * F, (t + 1) * F)

        def finish_rows(eng, g):
            step, steps = (last_step, 0) if eng is nc.vector else (row_step, g * 4)
            eng.wait_ge(pos_read, g * IT + IT)
            eng.wait_ge(neg_read, g * IT + IT)
            eng.tensor_tensor(pos_sum, pos_sum, neg_sum, ALU.add).then_inc(step, 1)
            eng.wait_ge(step, steps + 1)
            eng.tensor_tensor(joined, pos_sum[:, :, 0:HW], pos_sum[:, :, HW:VW], ALU.add).then_inc(joined_ready, 1)
            if eng is nc.vector:
                denominators(g)
            if not (isinstance(g, int) and g == 0):
                eng.wait_ge(out_landed, g * 16)
            eng.wait_ge(rden_ready, g + 1)
            eng.tensor_tensor(h.rearrange("p (t c) -> p t c", t=IT), joined[:, :, 0:F],
                              rden[:].rearrange("p (t k) -> p t k", k=1).to_broadcast([P, IT, F]),
                              ALU.mult).then_inc(h_ready, 1)
            if eng is nc.vector:
                minima(g)
            eng.wait_ge(min_ready, g + 1)
            eng.tensor_tensor(h, h, h_min, ALU.subtract).then_inc(step, 1)
            eng.wait_ge(x1_back_landed, g * 16 + 16)
            eng.wait_ge(step, steps + 2)
            eng.tensor_tensor(h, h, x1_back, ALU.add).then_inc(step, 1)
            eng.wait_ge(exp_ready, g + 1)
            eng.wait_ge(step, steps + 3)
            eng.tensor_tensor(h, h, h_exp, ALU.add).then_inc(res_ready, 1)
            if eng is nc.vector:
                row_moments(g)
            else:
                inverse_deviation(g)
            eng.wait_ge(moments2_ready, g * IT + IT)
            eng.tensor_tensor(h.rearrange("p (t c) -> p t c", t=IT), h.rearrange("p (t c) -> p t c", t=IT),
                              moments[:, :, 0:1].to_broadcast([P, IT, F]), ALU.subtract).then_inc(step, 1)
            eng.wait_ge(rstd2_ready, g + 1)
            eng.wait_ge(step, steps + 4)
            eng.tensor_tensor(h.rearrange("p (t c) -> p t c", t=IT), h.rearrange("p (t c) -> p t c", t=IT),
                              rstd[:].rearrange("p (t k) -> p t k", k=1).to_broadcast([P, IT, F]),
                              ALU.mult).then_inc(normed, 1)

        def denominators(g):
            nc.vector.wait_ge(joined_ready, g + 1)
            nc.vector.reciprocal(rden[:], joined[:, :, F]).then_inc(inv_ready, 1)
            nc.vector.wait_ge(inv_ready, g + 1)
            nc.vector.tensor_scalar(rden[:], rden[:], w_pow[:], None, ALU.mult).then_inc(rden_ready, 1)

        def minima(g):
            nc.vector.wait_ge(h_ready, g + 1)
            nc.vector.tensor_scalar(h_min, h, 0.0, None, ALU.min).then_inc(min_ready, 1)

        def row_moments(g):
            nc.vector.wait_ge(res_ready, g + 1)
            for t in range(IT):
                nc.vector.bn_stats(stats[:, t, :], h[:, rows(t)]).then_inc(stats2_ready, 1)
            for t in range(IT):
                nc.vector.wait_ge(stats2_ready, g * IT + (t + 1))
                nc.vector.sem_inc(held_vector, 1)
                nc.vector.bn_aggr(moments[:, t, :], stats[:, t, :]).then_inc(moments2_ready, 1)

        def inverse_deviation(g):
            nc.gpsimd.wait_ge(moments2_ready, g * IT + IT)
            nc.gpsimd.tensor_tensor(vare[:], moments[:, :, 1], eps_cols[:], ALU.add).then_inc(pool_step, 1)
            nc.gpsimd.wait_ge(pool_step, g + (NG + 1))
            nc.gpsimd.tensor_tensor(rstd[:], vare[:], minus_half[:], ALU.pow).then_inc(rstd2_ready, 1)

        @block.sync
        def _(sp):
            def load_chunk(g, c):
                s = c % SLOTS
                if not (isinstance(g, int) and c < SLOTS):
                    sp.wait_ge(a01_ready, g * NC + (c - SLOTS + 1))
                    sp.wait_ge(mask_ready, g * NC + (c - SLOTS + 1))
                sp.dma_start(adj_in[:, s, :],
                             adj_tiles[bass.ds(g, 1), :, c * CJ * GI:(c + 1) * CJ * GI].rearrange(
                                 "g p n -> (g p) n")).then_inc(adj_landed[s], 16)

            for c in range(NC):
                load_chunk(0, c)
            with sp.Fori(1, NG) as g:
                for c in range(NC):
                    load_chunk(g, c)

            def load_f1(g, odd):
                sp.dma_start(f1_rows[:, odd * GI:(odd + 1) * GI],
                             f1_dram[bass.ds(g, 1)].rearrange("g a n -> (g a) n").to_broadcast([P, GI])).then_inc(
                                 f1_landed[odd], 16)

            sp.wait_ge(f1_stored, 16 * 2)
            load_f1(0, 0)
            load_f1(1, 1)
            sp.wait_ge(chunk_used, NG * NC)
            sp.wait_ge(a01_ready, NG * NC)
            sp.wait_ge(mask_ready, NG * NC)
            sp.wait_ge(v_stored, 16 * LAST)
            for g in range(LAST):
                sp.dma_start(v_all[:, g * IT:(g + 1) * IT, :, :].rearrange("p t k c -> p (t k c)"),
                             v_dram[g]).then_inc(v_landed, 16)

            def group_dmas(g, odd, load):
                sp.wait_ge(res_ready, g)
                sp.dma_start(x1_back, x1_dram[bass.ds(g, 1)].rearrange("g p n -> (g p) n")).then_inc(
                    x1_back_landed, 16)
                sp.wait_ge(normed, g)
                sp.dma_start(out_tiles[:, bass.ds(g * IT - IT, IT), :].rearrange("p t c -> p (t c)"), h).then_inc(
                    out_landed, 16)
                if load:
                    sp.wait_ge(sign_ready, g * NT + NT)
                    load_f1(g + 2, odd)

            sp.wait_ge(x1_stored, 16 * NG)
            sp.wait_ge(f1_stored, 16 * NG)
            sp.wait_ge(f1_ready, NG)
            sp.dma_start(x1_back, x1_dram[0]).then_inc(x1_back_landed, 16)
            sp.wait_ge(sign_ready, NT)
            load_f1(2, 0)
            group_dmas(1, 1, True)
            with sp.Fori(1, NG // 2 - 1) as k:
                group_dmas(k * 2, 0, True)
                group_dmas(k * 2 + 1, 1, True)
            group_dmas(NG - 2, 0, False)
            group_dmas(NG - 1, 1, False)
            sp.wait_ge(normed, NG)
            sp.dma_start(out_tiles[:, LAST * IT:NG * IT, :].rearrange("p t c -> p (t c)"), h).then_inc(
                out_landed, 16)
            sp.wait_ge(out_landed, 16 * NG)

            sp.wait_ge(wide_known, 1)
            with sp.If(sp.value_load(is_wide[0:1, 0:1], min_val=0, max_val=1) > 0):
                with sp.Fori(0, NG) as g:
                    sp.dma_start(x1_back, x1_dram[bass.ds(g, 1)].rearrange("g p n -> (g p) n")).then_inc(
                        wide_x1_landed, 16)
                    sp.wait_ge(wide_turned, g + 1)
                    sp.sem_inc(held_sp, 1)
                with sp.Fori(0, NG) as g:
                    sp.dma_start(f1_rows[:, 0:GI],
                                 f1_dram[bass.ds(g, 1)].rearrange("g a n -> (g a) n").to_broadcast(
                                     [P, GI])).then_inc(wide_rows_landed, 16)
                    sp.dma_start(x1_back, x1_dram[bass.ds(g, 1)].rearrange("g p n -> (g p) n")).then_inc(
                        wide_rows_landed, 16)
                    sp.wait_ge(wide_normed, g + 1)
                    sp.sem_inc(held_sp, 1)
                    sp.dma_start(out_tiles[:, bass.ds(g * IT, IT), :].rearrange("p t c -> p (t c)"), h).then_inc(
                        wide_out_landed, 16)
                    sp.wait_ge(wide_out_landed, g * 16 + 16)
                    sp.sem_inc(held_sp, 1)

        @block.gpsimd
        def _(pool):
            nc.gpsimd.memset(ident[:], 1.0).then_inc(ident_ready, 1)
            pool.wait_ge(ident_ready, 1)
            nc.gpsimd.affine_select(out=ident[:], in_=ident[:], compare_op=ALU.is_equal, fill=0.0, base=0,
                                    pattern=[[-1, P]], channel_multiplier=1).then_inc(ident_ready, 1)
            nc.gpsimd.memset(minus_half[:], -0.5).then_inc(consts_ready, 1)
            nc.gpsimd.memset(eps_cols[:], EPS).then_inc(consts_ready, 1)
            nc.gpsimd.memset(wh[:, :, F:HW], 1.0).then_inc(consts_ready, 1)
            for k in range(NG):
                t = slice(k * IT, (k + 1) * IT)
                pool.wait_ge(x_hi_ready, k + 1)
                nc.gpsimd.tensor_tensor(x_rest[:, t, :], x_all[:, t, :], xparts[:, t, 0:F],
                                        ALU.subtract).then_inc(x_rest_ready, 1)
                pool.wait_ge(x_mid_ready, k + 1)
                nc.gpsimd.tensor_tensor(xparts[:, t, 2 * F:3 * F], x_rest[:, t, :], xparts[:, t, F:2 * F],
                                        ALU.subtract).then_inc(x_parts_ready, 1)
            pool.wait_ge(w_max_ready, 1)
            nc.gpsimd.partition_all_reduce(w_lim[:, 3:4], w_lim[:, 2:3], P, bass.bass_isa.ReduceOp.max).then_inc(
                w_all_ready, 1)

            def residual_rows(g):
                pool.dma_start(x_res, x_tiles[:, bass.ds(g * IT, IT), :].rearrange("p t c -> p (t c)")).then_inc(
                    xres_landed, 16)
                pool.wait_ge(xres_landed, g * 16 + 16)
                nc.gpsimd.tensor_tensor(x_res.rearrange("p (t c) -> p t c", t=IT),
                                        x_res.rearrange("p (t c) -> p t c", t=IT),
                                        b_rows[:].rearrange("p (t c) -> p t c", t=1).to_broadcast([P, IT, F]),
                                        ALU.add).then_inc(xb_ready, 1)

            def layer0_rows(g, last=False):
                pool.wait_ge(moments_ready, g * IT + IT)
                nc.gpsimd.tensor_tensor(vare[:], moments[:, :, 1], eps_cols[:], ALU.add).then_inc(pool_step, 1)
                pool.wait_ge(pool_step, g + 1)
                nc.gpsimd.tensor_tensor(rstd[:], vare[:], minus_half[:], ALU.pow).then_inc(rstd_ready, 1)
                if not last:
                    residual_rows(g + 1)
                pool.wait_ge(x1_ready, g * IT + IT)
                pool.dma_start(x1_dram[bass.ds(g, 1)].rearrange("g p n -> (g p) n"), node).then_inc(x1_stored, 16)
                pool.wait_ge(f1_copied, g + 1)
                pool.dma_start(f1_dram[bass.ds(g, 1)].rearrange("g a n -> (g a) n"), f1_out[:]).then_inc(
                    f1_stored, 16)
                if not last:
                    pool.wait_ge(v_lo_ready, g * 2 * IT + 2 * IT)
                    pool.dma_start(v_dram[bass.ds(g, 1)].rearrange("g p n -> (g p) n"),
                                   v_new.rearrange("p t k c -> p (t k c)")).then_inc(v_stored, 16)

            pool.wait_ge(w_landed, 16 * 5)
            residual_rows(0)
            with pool.Fori(0, LAST) as g:
                layer0_rows(g)
            layer0_rows(LAST, last=True)

            pool.wait_ge(lim_ready, 1)
            nc.gpsimd.partition_all_reduce(f_lim[:, 7:8], f_lim[:, 6:7], P, bass.bass_isa.ReduceOp.max).then_inc(
                lim_all_ready, 1)
            finish_rows(nc.gpsimd, 0)
            with pool.Fori(1, LAST) as g:
                finish_rows(nc.gpsimd, g)
            inverse_deviation(LAST)

            pool.wait_ge(wide_known, 1)
            with pool.If(pool.value_load(is_wide[0:1, 0:1], min_val=0, max_val=1) > 0):
                with pool.Fori(0, NG) as g:
                    pool.wait_ge(wide_best_ready, g + 1)
                    pool.sem_inc(held_pool, 1)
                    nc.gpsimd.partition_all_reduce(wide_max, wide_best, P, bass.bass_isa.ReduceOp.max).then_inc(
                        wide_max_ready, 1)
                    pool.wait_ge(wide_moments_ready, g + 1)
                    nc.gpsimd.tensor_tensor(vare[:], moments[:, :, 1], eps_cols[:], ALU.add).then_inc(
                        wide_pool_step, 1)
                    pool.wait_ge(wide_pool_step, g + 1)
                    nc.gpsimd.tensor_tensor(rstd[:], vare[:], minus_half[:], ALU.pow).then_inc(wide_rstd_ready, 1)

        @block.scalar
        def _(act):
            QX = NT // XQ
            for q in range(XQ):
                act.dma_start(x_all[:, q * QX:(q + 1) * QX, :], x_tiles[:, q * QX:(q + 1) * QX, :]).then_inc(
                    x_landed[q], 16)
            act.dma_start(w1_sb[:, 0:F], w1).then_inc(w_landed, 16)
            act.dma_start(w1t_sb[:], w1t).then_inc(w_landed, 16)
            act.dma_start(w0t_sb[:], w0t).then_inc(w_landed, 16)
            act.dma_start(a_sb[:], a_cols).then_inc(w_landed, 16)
            act.dma_start(b_rows[:], b0.to_broadcast([P, F])).then_inc(w_landed, 16)

            def keep_mask(g, c):
                act.wait_ge(adj_landed[c % SLOTS], g * 16 * LAPS + 16 * (c // SLOTS + 1))
                nc.scalar.activation(
                    mask[:, bass.ds(g, 1), c * CJ * GW:(c + 1) * CJ * GW].rearrange("p g n -> p (g n)").bitcast(I8),
                    adj_in[:, c % SLOTS, :], ACT.Sign, bias=half[:], scale=-1.0).then_inc(mask_ready, 1)

            def weights_of_nodes(g):
                act.wait_ge(f_copied, g * IT + IT)
                f2 = f_cols[:, bass.ds(g * IT, IT), 1:2].rearrange("p t k -> p (t k)")
                nc.scalar.activation(weight[:, :, 0], f2, ACT.Exp)
                nc.scalar.activation(weight[:, :, 1], f2, ACT.Exp, scale=ALPHA).then_inc(weight_ready, 1)

            def high_parts(g, t, v, first=False):
                if t == 0:
                    act.wait_ge(mant_ready, g + 1)
                    act.wait_ge(wh_copied, g * IT + IT)
                    if v is v_new and not first:
                        act.wait_ge(v_stored, g * 16)
                for k in range(2):
                    nc.scalar.activation(v[:, t, k, 0:HW], wh[:, t, :], ACT.Copy,
                                         scale=mant[:, t, k:k + 1]).then_inc(v_hi_ready, 1)

            act.wait_ge(consts_ready, 4)
            for c in range(NC):
                keep_mask(0, c)

            def group(g, first=False):
                for c in range(NC):
                    keep_mask(g, c)
                    if c == 11:
                        weights_of_nodes(g - 1)
                    if c >= 12:
                        high_parts(g - 1, c - 12, v_new, first)

            act.wait_ge(x_parts_ready, NG)
            group(1, True)
            with act.Fori(2, NG) as g:
                group(g)
            weights_of_nodes(LAST)
            for t in range(IT):
                high_parts(LAST, t, v_all[:, LAST * IT:NG * IT])

            act.wait_ge(row_arg_ready, 2)
            nc.scalar.activation(row_fac[:], row_arg[:], ACT.Exp).then_inc(row_fac_ready, 1)
            act.wait_ge(row_fac_ready, 1)

            def sign_tile(g, odd, jt):
                s = jt % RING
                if jt == 0 and isinstance(g, int):
                    act.wait_ge(f1_landed[odd], 16)
                elif jt == 0:
                    act.wait_ge(f1_landed[odd], (g - odd) * 8 + 16)
                if not (isinstance(g, int) and g == 0 and jt < RING):
                    act.wait_ge(not_pos_ready, g * NT + (jt - RING + 1))
                nc.scalar.activation(sign[:, s, :].bitcast(I8), f1_rows[:, odd * GI:(odd + 1) * GI], ACT.Sign,
                                     bias=thr[:, jt:jt + 1], scale=-1.0).then_inc(sign_ready, 1)

            def read_positive(g, first=False):
                for t in range(IT):
                    acc_done(act, g, t)
                    if t == 0 and not first:
                        act.wait_ge(joined_ready, g)
                    nc.scalar.activation(pos_sum[:, t, :], acc[:, 2 * t, 0:VW], ACT.Copy,
                                         scale=row_fac[:, 0, bass.ds(g * IT + t, 1)]).then_inc(pos_read, 1)

            def elu_exp(g):
                act.wait_ge(min_ready, g + 1)
                nc.scalar.activation(h_exp, h_min, ACT.Exp).then_inc(elu_ready, 1)
                act.wait_ge(elu_ready, g + 1)
                nc.scalar.activation(h_exp, h_exp, ACT.Copy, bias=-1.0).then_inc(exp_ready, 1)

            def group1(g, odd, tail=True, first=False):
                for jt in range(NT):
                    sign_tile(g, odd, jt)
                    if tail and jt == 1:
                        read_positive(g - 1, first)
                    if tail and jt == 14:
                        elu_exp(g - 1)

            act.wait_ge(x1_stored, 16 * NG)
            group1(0, 0, tail=False)
            group1(1, 1, first=True)
            with act.Fori(1, NG // 2) as k:
                group1(k * 2, 0)
                group1(k * 2 + 1, 1)
            read_positive(LAST)
            elu_exp(LAST)

            act.wait_ge(wide_known, 1)
            with act.If(act.value_load(is_wide[0:1, 0:1], min_val=0, max_val=1) > 0):
                with act.Fori(0, NG) as g:
                    with act.Fori(0, NT) as jt:
                        act.wait_ge(wide_arg_ready, g * NT + jt + 1)
                        nc.scalar.activation(wide_prob, wide_sum, ACT.Exp).then_inc(wide_exp_ready, 1)
                    act.wait_ge(wide_min_ready, g + 1)
                    nc.scalar.activation(h_exp, h_min, ACT.Exp).then_inc(wide_elu_ready, 1)

        @block.tensor
        def _(pe):
            pe.wait_ge(w_landed, 16 * 5)
            nc.tensor.matmul(wa_ps, w1t_sb[:], a_sb[:], start=True, stop=True).then_inc(wa_ready, 1)

            def chunk(g, c):
                pe.wait_ge(a01_ready, g * NC + (c + 1))
                if isinstance(g, int) and c % 2 == 0:
                    pe.wait_ge(x_parts_ready, c // 2 + 1)
                for j in range(CJ):
                    jt = c * CJ + j
                    for t in range(IT):
                        if jt == 0 and not isinstance(g, int):
                            pe.wait_ge(sums_read, g * IT + (t - IT + 1))
                        mm = nc.tensor.matmul(sums[:, t, 0:XW],
                                              a01[:, c % SLOTS, j * GI + t * P:j * GI + (t + 1) * P],
                                              xparts[:, jt, :], start=(jt == 0), stop=(jt == NT - 1))
                        if j == CJ - 1 and t == IT - 1:
                            mm.then_inc(chunk_used, 1)
                        elif jt == NT - 1:
                            mm.then_inc(sums_ready, 1)

            def turn_sums(g):
                for t in range(IT):
                    pe.wait_ge(sums_read, g * IT + (t + 1))
                    nc.tensor.transpose(agg_t_ps[:, t * P:(t + 1) * P], node[:, rows(t)], ident[:]).then_inc(
                        agg_t_ready, 1)

            def linear(g):
                for t in range(IT):
                    pe.wait_ge(agg_t_copied, g * IT + (t + 1))
                    nc.tensor.matmul(lin_ps[:, rows(t)], node_t[:, t * P:(t + 1) * P], w0t_sb[:],
                                     start=True, stop=True).then_inc(lin_ready, 1)

            def turn_x1(g):
                for t in range(IT):
                    pe.wait_ge(x1_ready, g * IT + (t + 1))
                    nc.tensor.transpose(x1_t_ps[:, t * P:(t + 1) * P], node[:, rows(t)], ident[:]).then_inc(
                        x1_t_ready, 1)

            def project(g):
                pe.wait_ge(x1_t_copied, g * IT + IT)
                for t in range(IT):
                    nc.tensor.matmul(wh_ps[:, t // 2, t % 2, :], node_t[:, t * P:(t + 1) * P], w1_sb[:],
                                     start=True, stop=True).then_inc(wh_ready, 1)
                nc.tensor.matmul(f1_ps, wa_wide[:], node_t, start=True, stop=True).then_inc(f1_ready, 1)

            pe.wait_ge(ident_ready, 2)
            for c in range(NC):
                chunk(0, c)
            pe.wait_ge(weights_ready, 1)
            with pe.Fori(1, NG) as g:
                for c in range(NC):
                    chunk(g, c)
                    if c == 0:
                        turn_sums(g - 1)
                    if c == 2:
                        linear(g - 1)
                    if c == 6:
                        turn_x1(g - 1)
                    if c == 8:
                        project(g - 1)
            turn_sums(LAST)
            linear(LAST)
            turn_x1(LAST)
            project(LAST)

            def alone():
                pe.sem_inc(held_pe, 1)

            def tile(g, jt):
                start, stop, s = jt == 0, jt == NT - 1, jt % RING
                if isinstance(g, int) and jt == LAST * IT:
                    pe.wait_ge(v_lo_ready, NG * 2 * IT)
                pe.wait_ge(pos_ready, g * NT + (jt + 1))
                pe.wait_ge(neg_ready, g * NT + (jt + 1))
                alone()
                for t in range(IT):
                    for k, (tiles, read) in enumerate(((n_pos, pos_read), (n_neg, neg_read))):
                        if start and not isinstance(g, int):
                            pe.wait_ge(read, g * IT + (t + 1 - IT))
                            alone()
                        mm = nc.tensor.matmul(acc[:, 2 * t + k, 0:VW],
                                              tiles[:, s, t * P // 4:(t + 1) * P // 4].bitcast(F8),
                                              v_all[:, jt, k, :], start=start, stop=stop)
                    if t == IT - 1:
                        mm.then_inc(tile_used, 1)
                    elif stop:
                        mm.then_inc(acc_ready, 1)

            pe.wait_ge(wh_copied, NG * IT)
            pe.wait_ge(f1_copied, NG)
            pe.wait_ge(v_landed, 16 * LAST)
            for jt in range(NT):
                tile(0, jt)
            with pe.Fori(1, NG) as g:
                for jt in range(NT):
                    tile(g, jt)

            pe.wait_ge(wide_known, 1)
            with pe.If(pe.value_load(is_wide[0:1, 0:1], min_val=0, max_val=1) > 0):
                pe.wait_ge(out_landed, 16 * NG)
                with pe.Fori(0, NG) as g:
                    pe.wait_ge(wide_x1_landed, g * 16 + 16)
                    alone()
                    for t in range(IT):
                        mm = nc.tensor.transpose(wide_turned_ps[:, t * P:(t + 1) * P], x1_back[:, rows(t)], ident[:])
                    mm.then_inc(wide_turned, 1)
                    pe.wait_ge(wide_turned_copied, g + 1)
                    alone()
                    for t in range(IT):
                        mm = nc.tensor.matmul(wide_wh_ps[:, rows(t)], h_min[:, t * P:(t + 1) * P], w1_sb[:, 0:F],
                                              start=True, stop=True)
                    mm.then_inc(wide_wh_made, 1)
                    pe.wait_ge(wide_wh_copied, g + 1)
                    alone()
                with pe.Fori(0, NG) as g:
                    with pe.Fori(0, NT) as jt:
                        pe.wait_ge(wide_prob_ready, g * NT + jt + 1)
                        alone()
                        for t in range(IT):
                            mm = nc.tensor.matmul(wide_part[:, t, :], wide_prob[:, t * P:(t + 1) * P],
                                                  wide_wh[:, bass.ds(jt, 1), :].rearrange("p t c -> p (t c)"),
                                                  start=True, stop=True)
                        mm.then_inc(wide_part_ready, 1)
                        pe.wait_ge(wide_part_added, g * NT + jt + 1)
                        alone()

        @block.vector
        def _(dve):
            def alone():
                dve.sem_inc(held_vector, 1)

            nc.vector.memset(half[:], 0.5).then_inc(consts_ready, 1)
            nc.vector.memset(xparts[:, :, 3 * F:XW], 1.0).then_inc(w_step, 1)

            def high_part(k):
                t = slice(k * IT, (k + 1) * IT)
                dve.wait_ge(x_landed[k * XQ // NG], 16)
                nc.vector.tensor_copy(xparts[:, t, 0:F], x_all[:, t, :]).then_inc(x_hi_ready, 1)

            def middle_part(k):
                t = slice(k * IT, (k + 1) * IT)
                dve.wait_ge(x_rest_ready, k + 1)
                nc.vector.tensor_copy(xparts[:, t, F:2 * F], x_rest[:, t, :]).then_inc(x_mid_ready, 1)

            def binarise(g, c):
                s = c % SLOTS
                dve.wait_ge(adj_landed[s], g * 16 * LAPS + 16 * (c // SLOTS + 1))
                if not (isinstance(g, int) and g == 0 and c < SLOTS):
                    dve.wait_ge(chunk_used, g * NC + (c - SLOTS + 1))
                nc.vector.tensor_scalar(a01[:, s, :], adj_in[:, s, :], 1.0, None, ALU.is_equal).then_inc(a01_ready, 1)

            high_part(0)
            high_part(1)
            for c in range(NC):
                if c % 2 == 0:
                    middle_part(c // 2)
                    if c // 2 + 2 < NG:
                        high_part(c // 2 + 2)
                binarise(0, c)

            dve.wait_ge(w_landed, 16 * 5)
            nc.vector.tensor_reduce(w_lim[:, 0:1], w1_sb[:, 0:F], AX.X, ALU.max).then_inc(w_step, 1)
            nc.vector.tensor_reduce(w_lim[:, 1:2], w1_sb[:, 0:F], AX.X, ALU.min).then_inc(w_step, 1)
            dve.wait_ge(w_step, 3)
            nc.vector.scalar_tensor_tensor(w_lim[:, 2:3], w_lim[:, 1:2], -1.0, w_lim[:, 0:1], ALU.mult,
                                           ALU.max).then_inc(w_max_ready, 1)
            dve.wait_ge(w_all_ready, 1)
            nc.vector.tensor_scalar(w_lim[:, 2:3], w_lim[:, 3:4], 1e-30, 1e37, ALU.max, ALU.min).then_inc(w_step, 1)
            dve.wait_ge(w_step, 4)
            nc.vector.tensor_scalar(w_pow[:].bitcast(I32), w_lim[:, 2:3].bitcast(I32), EXP_BITS, None,
                                    ALU.bitwise_and).then_inc(w_step, 1)
            dve.wait_ge(w_step, 5)
            nc.vector.reciprocal(w_inv[:], w_pow[:]).then_inc(w_step, 1)
            dve.wait_ge(w_step, 6)
            nc.vector.tensor_scalar(w1_sb[:, 0:F], w1_sb[:, 0:F], w_inv[:], None, ALU.mult).then_inc(w_step, 1)
            dve.wait_ge(wa_ready, 1)
            nc.vector.tensor_copy(w1_sb[:, F:F + 2], wa_ps).then_inc(w_step, 1)
            dve.wait_ge(w_step, 8)
            nc.vector.tensor_copy(wa_wide[:], w1_sb[:, F:F + 1].to_broadcast([P, P])).then_inc(weights_ready, 1)

            def read_sums(g, first=False):
                if not first:
                    dve.wait_ge(x1_stored, g * 16)
                for t in range(IT):
                    sums_done(dve, g, t)
                    nc.vector.tensor_reduce(node[:, rows(t)],
                                            sums[:, t, 0:3 * F].rearrange("p (k f) -> p f k", k=3),
                                            AX.X, ALU.add)
                    nc.vector.reciprocal(rdeg[:, t:t + 1], sums[:, t, 3 * F:XW]).then_inc(sums_read, 1)

            def copy_turned(dst, src, ready, done, g):
                dve.wait_ge(ready, g * IT + IT)
                nc.vector.tensor_copy(dst, src).then_inc(done, IT)

            def residual(g):
                dve.wait_ge(xb_ready, g + 1)
                dve.wait_ge(lin_ready, g * IT + IT)
                for t in range(IT):
                    nc.vector.scalar_tensor_tensor(node[:, rows(t)], lin_ps[:, rows(t)], rdeg[:, t:t + 1],
                                                   x_res[:, rows(t)], ALU.mult, ALU.add).then_inc(y_ready, 1)

            def y_moments(g):
                for t in range(IT):
                    dve.wait_ge(y_ready, g * IT + (t + 1))
                    nc.vector.bn_stats(stats[:, t, :], node[:, rows(t)]).then_inc(stats_ready, 1)
                for t in range(IT):
                    dve.wait_ge(stats_ready, g * IT + (t + 1))
                    alone()
                    nc.vector.bn_aggr(moments[:, t, :], stats[:, t, :]).then_inc(moments_ready, 1)

            def normalise(g):
                dve.wait_ge(rstd_ready, g + 1)
                for t in range(IT):
                    nc.vector.tensor_scalar(node[:, rows(t)], node[:, rows(t)], moments[:, t, 0:1],
                                            rstd[:, t:t + 1], ALU.subtract, ALU.mult).then_inc(x1_ready, 1)

            def take_f(g):
                dve.wait_ge(wh_ready, g * IT + IT)
                fc = f_cols[:, bass.ds(g * IT, IT), :]
                nc.vector.tensor_copy(fc.rearrange("p (b t) c -> p b t c", b=2), wh_ps[:, :, :, F:F + 2]).then_inc(
                    f_copied, IT)
                nc.vector.tensor_copy(wh[:, :, 0:F].rearrange("p (b t) c -> p b t c", b=2),
                                      wh_ps[:, :, :, 0:F]).then_inc(wh_copied, IT)

            def take_f1(g, first=False):
                if not first:
                    dve.wait_ge(f1_stored, g * 16)
                dve.wait_ge(f1_ready, g + 1)
                nc.vector.tensor_copy(f1_out[:], f1_ps[0:1, :]).then_inc(f1_copied, 1)

            def split_weights(g):
                dve.wait_ge(f_copied, g * IT + IT)
                nc.vector.tensor_scalar(thr[:, bass.ds(g * IT, IT)],
                                        f_cols[:, bass.ds(g * IT, IT), 1:2].rearrange("p t k -> p (t k)"),
                                        -1.0, None, ALU.mult)
                base = g * 4
                dve.wait_ge(weight_ready, g + 1)
                nc.vector.tensor_scalar(w_exp[:, 0], weight[:].bitcast(I32), 23, None,
                                        ALU.logical_shift_right).then_inc(w_bits, 1)
                dve.wait_ge(w_bits, base + 1)
                nc.vector.tensor_scalar(w_exp[:, 1], w_exp[:, 0], float(F8_LOW), float(F8_HIGH), ALU.max,
                                        ALU.min).then_inc(w_bits, 1)
                dve.wait_ge(w_bits, base + 2)
                nc.vector.tensor_scalar(w_unit[:, 0], w_exp[:, 1], -1.0, float(2 * F32_BIAS + MANT_SHIFT), ALU.mult,
                                        ALU.add).then_inc(w_bits, 1)
                nc.vector.tensor_scalar(
                    power[:, bass.ds(g * IT * 2, IT * 2), :],
                    w_exp[:, 1].rearrange("p t (k o) -> p (t k) o", o=1).to_broadcast([P, IT * 2, 4]),
                    float(F8_BIAS - F32_BIAS), 4.0, ALU.add, ALU.mult)
                dve.wait_ge(w_bits, base + 3)
                nc.vector.tensor_scalar(w_unit[:, 1], w_unit[:, 0], 23, None,
                                        ALU.logical_shift_left).then_inc(w_bits, 1)
                dve.wait_ge(w_bits, base + 4)
                nc.vector.tensor_tensor(mant[:], weight[:], w_unit[:, 1].bitcast(F32), ALU.mult).then_inc(
                    mant_ready, 1)

            def low_parts(g, t, v):
                for k in range(2):
                    dve.wait_ge(v_hi_ready, g * 2 * IT + (2 * t + k + 1))
                    nc.vector.scalar_tensor_tensor(v[:, t, k, HW:VW], wh[:, t, :], mant[:, t, k:k + 1],
                                                   v[:, t, k, 0:HW], ALU.mult, ALU.subtract).then_inc(v_lo_ready, 1)

            def group(g, first=False):
                m = g - 1
                for c in range(NC):
                    binarise(g, c)
                    if c == 0:
                        read_sums(m, first)
                    if c == 2:
                        copy_turned(node_t, agg_t_ps, agg_t_ready, agg_t_copied, m)
                    if c == 4:
                        residual(m)
                    if c == 5:
                        y_moments(m)
                    if c == 7:
                        normalise(m)
                    if c == 9:
                        copy_turned(node_t, x1_t_ps, x1_t_ready, x1_t_copied, m)
                    if c == 11:
                        take_f(m)
                    if c == 12:
                        take_f1(m, first)
                        split_weights(m)
                    if c >= 14:
                        low_parts(m, c - 14, v_new)
                low_parts(m, 2, v_new)
                low_parts(m, 3, v_new)

            group(1, True)
            with dve.Fori(2, NG) as g:
                group(g)
            read_sums(LAST)
            copy_turned(node_t, agg_t_ps, agg_t_ready, agg_t_copied, LAST)
            residual(LAST)
            y_moments(LAST)
            normalise(LAST)
            copy_turned(node_t, x1_t_ps, x1_t_ready, x1_t_copied, LAST)
            take_f(LAST)
            split_weights(LAST)
            take_f1(LAST)
            for t in range(IT):
                low_parts(LAST, t, v_all[:, LAST * IT:NG * IT])

            for k in range(2):
                f = f_cols[:, :, k]
                nc.vector.tensor_reduce(f_lim[:, 3 * k:3 * k + 1], f, AX.X, ALU.max).then_inc(lim_step, 1)
                nc.vector.tensor_reduce(f_lim[:, 3 * k + 1:3 * k + 2], f, AX.X, ALU.min).then_inc(lim_step, 1)
            dve.wait_ge(lim_step, 4)
            for k in range(2):
                nc.vector.scalar_tensor_tensor(f_lim[:, 3 * k + 2:3 * k + 3], f_lim[:, 3 * k + 1:3 * k + 2], -1.0,
                                               f_lim[:, 3 * k:3 * k + 1], ALU.mult, ALU.max).then_inc(lim_step, 1)
            dve.wait_ge(lim_step, 6)
            nc.vector.scalar_tensor_tensor(f_lim[:, 6:7], f_lim[:, 2:3], F2_LIMIT / F1_LIMIT, f_lim[:, 5:6],
                                           ALU.mult, ALU.max).then_inc(lim_ready, 1)

            nc.vector.tensor_scalar(row_arg[:, 0, :], f_cols[:, :, 0], 0.0, 1.0 - ALPHA, ALU.min,
                                    ALU.mult).then_inc(row_arg_ready, 1)
            nc.vector.tensor_scalar(row_arg[:, 1, :], f_cols[:, :, 0], 0.0, ALPHA - 1.0, ALU.max,
                                    ALU.mult).then_inc(row_arg_ready, 1)
            dve.wait_ge(row_arg_ready, 2)

            def pattern(jt, k):
                return power[:, 2 * jt + k, :].bitcast(I32)

            def masks(g, jt):
                return mask[:, bass.ds(g, 1), jt * GW:(jt + 1) * GW].rearrange("p g n -> p (g n)")

            def positive_tile(g, jt):
                dve.wait_ge(sign_ready, g * NT + (jt + 1))
                if not (isinstance(g, int) and g == 0 and jt < RING):
                    dve.wait_ge(tile_used, g * NT + (jt - RING + 1))
                nc.vector.scalar_tensor_tensor(n_pos[:, jt % RING, :], sign[:, jt % RING, :], pattern(jt, 0),
                                               masks(g, jt), ALU.bitwise_and, ALU.bitwise_and).then_inc(
                                                   pos_ready, 1)

            def not_positive_tile(g, jt):
                nc.vector.scalar_tensor_tensor(not_pos[:, jt % 2, :], sign[:, jt % RING, :], -1, masks(g, jt),
                                               ALU.bitwise_xor, ALU.bitwise_and).then_inc(not_pos_ready, 1)

            def negative_tile(g, jt):
                dve.wait_ge(not_pos_ready, g * NT + (jt + 1))
                nc.vector.tensor_scalar(n_neg[:, jt % RING, :], not_pos[:, jt % 2, :], pattern(jt, 1), None,
                                        ALU.bitwise_and).then_inc(neg_ready, 1)

            def read_negative(g, first=False):
                for t in range(IT):
                    acc_done(dve, g, t)
                    if t == 0 and not first:
                        dve.wait_ge(joined_ready, g)
                    nc.vector.tensor_scalar(neg_sum[:, t, :], acc[:, 2 * t + 1, 0:VW],
                                            row_fac[:, 1, bass.ds(g * IT + t, 1)], None, ALU.mult).then_inc(
                                                neg_read, 1)

            def group1(g, tail=True, first=False):
                for jt in range(NT):
                    not_positive = jt
                    positive_tile(g, jt)
                    if jt > 0:
                        negative_tile(g, jt - 1)
                    not_positive_tile(g, not_positive)
                    if tail and jt == 2:
                        read_negative(g - 1, first)
                    if tail and jt == 9:
                        denominators(g - 1)
                    if tail and jt == 12:
                        minima(g - 1)
                    if tail and jt == 21:
                        row_moments(g - 1)
                negative_tile(g, NT - 1)

            def wide_rows():
                dve.wait_ge(out_landed, 16 * NG)
                nc.vector.memset(wide_wh[:, :, F:HW], 1.0)
                with dve.Fori(0, NG) as g:
                    dve.wait_ge(wide_turned, g + 1)
                    nc.vector.tensor_copy(h_min, wide_turned_ps).then_inc(wide_turned_copied, 1)
                    dve.wait_ge(wide_wh_made, g + 1)
                    nc.vector.tensor_copy(wide_wh[:, bass.ds(g * IT, IT), 0:F],
                                          wide_wh_ps.rearrange("p (t c) -> p t c", t=IT)).then_inc(wide_wh_copied, 1)

                FIND, SUM, END = 4, 5, 10
                STEPS = 2 + NT * FIND + 2 + NT * SUM + END

                def is_neighbour(g, jt):
                    return nc.vector.tensor_scalar(
                        wide_is, mask[:, bass.ds(g, 1), bass.ds(jt * GW, GW)].rearrange("p g n -> p (g n)").bitcast(I8),
                        0.0, -1.0, ALU.min, ALU.mult)

                def f2_col(jt):
                    return f_cols[:, bass.ds(jt, 1), 1:2].rearrange("p t k -> p (t k)")

                with dve.Fori(0, NG) as g:
                    n = g * STEPS
                    nc.vector.memset(wide_best, -WIDE).then_inc(wide_step, 1)
                    nc.vector.memset(wide_total, 0.0).then_inc(wide_step, 1)
                    n = n + 2
                    with dve.Fori(0, NT) as jt:
                        m = n + jt * FIND
                        dve.wait_ge(wide_step, m)
                        is_neighbour(g, jt).then_inc(wide_step, 1)
                        dve.wait_ge(wide_step, m + 1)
                        nc.vector.tensor_scalar(wide_cand, wide_is, -1.0, WIDE, ALU.add, ALU.mult).then_inc(
                            wide_step, 1)
                        dve.wait_ge(wide_step, m + 2)
                        nc.vector.scalar_tensor_tensor(wide_cand, wide_is, f2_col(jt), wide_cand, ALU.mult,
                                                       ALU.add).then_inc(wide_step, 1)
                        dve.wait_ge(wide_step, m + 3)
                        nc.vector.tensor_tensor(wide_best, wide_best, wide_cand, ALU.max).then_inc(wide_step, 1)
                    n = n + NT * FIND
                    dve.wait_ge(wide_step, n)
                    dve.sem_inc(wide_best_ready, 1)
                    dve.wait_ge(wide_rows_landed, g * 32 + 32)
                    dve.wait_ge(wide_max_ready, g + 1)
                    nc.vector.tensor_tensor(wide_max, wide_max, f1_rows[:, 0:GI], ALU.add).then_inc(wide_step, 1)
                    dve.wait_ge(wide_step, n + 1)
                    nc.vector.scalar_tensor_tensor(wide_max, wide_max, ALPHA, wide_max, ALU.mult,
                                                   ALU.max).then_inc(wide_step, 1)
                    n = n + 2
                    with dve.Fori(0, NT) as jt:
                        m = n + jt * SUM
                        dve.wait_ge(wide_step, m)
                        is_neighbour(g, jt)
                        nc.vector.tensor_scalar(wide_sum, f1_rows[:, 0:GI], f2_col(jt), None, ALU.add).then_inc(
                            wide_step, 1)
                        dve.wait_ge(wide_step, m + 1)
                        nc.vector.scalar_tensor_tensor(wide_sum, wide_sum, ALPHA, wide_sum, ALU.mult,
                                                       ALU.max).then_inc(wide_step, 1)
                        dve.wait_ge(wide_step, m + 2)
                        nc.vector.tensor_tensor(wide_sum, wide_sum, wide_max, ALU.subtract).then_inc(wide_step, 1)
                        dve.wait_ge(wide_step, m + 3)
                        nc.vector.tensor_scalar(wide_sum, wide_sum, 0.0, None, ALU.min).then_inc(wide_arg_ready, 1)
                        dve.wait_ge(wide_exp_ready, g * NT + jt + 1)
                        nc.vector.tensor_tensor(wide_prob, wide_prob, wide_is, ALU.mult).then_inc(wide_prob_ready, 1)
                        dve.wait_ge(wide_part_ready, g * NT + jt + 1)
                        nc.vector.tensor_tensor(wide_total, wide_total, wide_part, ALU.add).then_inc(
                            wide_part_added, 1)
                        dve.wait_ge(wide_part_added, g * NT + jt + 1)
                        dve.sem_inc(wide_step, 2)
                    n = n + NT * SUM
                    rows3 = h.rearrange("p (t c) -> p t c", t=IT)
                    dve.wait_ge(wide_step, n)
                    nc.vector.reciprocal(rden[:], wide_total[:, :, F]).then_inc(wide_step, 1)
                    dve.wait_ge(wide_step, n + 1)
                    nc.vector.tensor_scalar(rden[:], rden[:], w_pow[:], None, ALU.mult).then_inc(wide_step, 1)
                    dve.wait_ge(wide_step, n + 2)
                    nc.vector.tensor_tensor(rows3, wide_total[:, :, 0:F],
                                            rden[:].rearrange("p (t k) -> p t k", k=1).to_broadcast([P, IT, F]),
                                            ALU.mult).then_inc(wide_step, 1)
                    dve.wait_ge(wide_step, n + 3)
                    nc.vector.tensor_scalar(h_min, h, 0.0, None, ALU.min).then_inc(wide_min_ready, 1)
                    dve.wait_ge(wide_elu_ready, g + 1)
                    nc.vector.tensor_scalar(h_exp, h_exp, -1.0, None, ALU.add).then_inc(wide_step, 1)
                    nc.vector.tensor_tensor(h, h, h_min, ALU.subtract).then_inc(wide_step, 1)
                    dve.wait_ge(wide_step, n + 5)
                    nc.vector.tensor_tensor(h, h, x1_back, ALU.add).then_inc(wide_step, 1)
                    dve.wait_ge(wide_step, n + 6)
                    nc.vector.tensor_tensor(h, h, h_exp, ALU.add).then_inc(wide_step, 1)
                    dve.wait_ge(wide_step, n + 7)
                    alone()
                    for t in range(IT):
                        b = nc.vector.bn_stats(stats[:, t, :], h[:, rows(t)])
                    b.then_inc(wide_step, 1)
                    dve.wait_ge(wide_step, n + 8)
                    alone()
                    for t in range(IT):
                        b = nc.vector.bn_aggr(moments[:, t, :], stats[:, t, :])
                    b.then_inc(wide_moments_ready, 1)
                    dve.wait_ge(wide_moments_ready, g + 1)
                    nc.vector.tensor_tensor(rows3, rows3, moments[:, :, 0:1].to_broadcast([P, IT, F]),
                                            ALU.subtract).then_inc(wide_step, 1)
                    dve.wait_ge(wide_rstd_ready, g + 1)
                    dve.wait_ge(wide_step, n + 9)
                    nc.vector.tensor_tensor(rows3, rows3,
                                            rstd[:].rearrange("p (t k) -> p t k", k=1).to_broadcast([P, IT, F]),
                                            ALU.mult).then_inc(wide_normed, 1)
                    dve.wait_ge(wide_normed, g + 1)
                    dve.sem_inc(wide_step, 1)

            dve.wait_ge(row_fac_ready, 1)
            group1(0, tail=False)
            group1(1, first=True)
            dve.wait_ge(lim_all_ready, 1)
            nc.vector.tensor_scalar(is_wide[:], f_lim[:, 7:8], F2_LIMIT, None, ALU.is_gt).then_inc(wide_known, 1)
            with dve.Fori(2, NG) as g:
                group1(g)
            read_negative(LAST)
            finish_rows(nc.vector, LAST)

            dve.wait_ge(wide_known, 1)
            with dve.If(dve.value_load(is_wide[0:1, 0:1], min_val=0, max_val=1) > 0):
                wide_rows()


def kernel(x, adj, L0_gnn_W, L0_gnn_b, L1_gnn_W, L1_gnn_a):
    import numpy as np
    import concourse.bacc as bacc
    from concourse.bass_utils import run_bass_kernel_spmd

    adj_t = np.asarray(adj).T.reshape(NT, P, NG, GI).transpose(2, 1, 0, 3).reshape(NG, P, NT * GI)
    arrays = {
        "x_tiles": np.asarray(x).reshape(NT, P, F).transpose(1, 0, 2),
        "adj_tiles": adj_t,
        "w0t": np.asarray(L0_gnn_W).T,
        "b0": np.asarray(L0_gnn_b).reshape(1, F),
        "w1": np.asarray(L1_gnn_W),
        "w1t": np.asarray(L1_gnn_W).T,
        "a_cols": np.asarray(L1_gnn_a).reshape(2, F).T,
    }
    arrays = {k: np.ascontiguousarray(v) for k, v in arrays.items()}
    nc = bacc.Bacc("TRN2", target_bir_lowering=False, num_devices=1)
    args = [nc.dram_tensor(k, v.shape, mybir.dt.from_np(v.dtype), kind="ExternalInput").ap()
            for k, v in arrays.items()]
    out = nc.dram_tensor("out_tiles", (P, NT, F), F32, kind="ExternalOutput").ap()
    build(nc, *args, out)
    r = run_bass_kernel_spmd(nc, [arrays], core_ids=[0])
    got = r.results[0]["out_tiles"]
    return np.ascontiguousarray(got.transpose(1, 0, 2).reshape(N, F))
```

```python
from contextlib import ExitStack

import concourse.bass as bass
from concourse import mybir

ALU = mybir.AluOpType
ACT = mybir.ActivationFunctionType
AX = mybir.AxisListType
F32, BF16, F16, F8 = mybir.dt.float32, mybir.dt.bfloat16, mybir.dt.float16, mybir.dt.float8e5
I32, I8 = mybir.dt.int32, mybir.dt.int8

P = 128
N = 4096
F = 128
NT = N // P
GI = 512
NG = N // GI
IT = GI // P
CJ = 2
NC = NT // CJ
SLOTS = 4
LAPS = NC // SLOTS
XW = 3 * F + 1
HW = F + 1
VW = 2 * HW
RING = 8
BLOCK = 2
GW = GI // 4
EPS = 1e-5
ALPHA = 0.2
EXP_BITS = 0x7F800000
F32_BIAS, F8_BIAS = 127, 15
F8_LOW, F8_HIGH = F32_BIAS - 14, F32_BIAS + 15
EARLY = 4
F1_LIMIT, F2_LIMIT = 40.0, 9.5
F1_HELD, F2_HELD = 50.0, 10.0
WIDE = 3e38
MANT_SHIFT = 2


def build(nc, x_tiles, adj_tiles, w0t, b0, w1, w1t, a_cols, out_tiles):
    ctx = ExitStack()
    with ctx:
        def sb(name, shape, dt):
            return ctx.enter_context(nc.sbuf_tensor(name, shape, dt))

        def sem(name):
            return ctx.enter_context(nc.semaphore(name))

        x1_dram = nc.dram_tensor("x1_scratch", [NG, P, IT * F], F32, kind="Internal").ap()
        f1_dram = nc.dram_tensor("f1_scratch", [NG, 1, GI], F32, kind="Internal").ap()
        v_dram = nc.dram_tensor("v_scratch", [NG - 2, P, IT * 2 * VW], F16, kind="Internal").ap()

        mask = sb("mask", [P, NG, NT * GW], I32)
        arena_a = sb("arena_a", [P, NT * XW + SLOTS * CJ * GI * 2], BF16)
        arena_b = sb("arena_b", [P, 3 * RING * GW], I32)
        arena_c = sb("arena_c", [P, 3096], F32)
        xparts = arena_a[:, 0:NT * XW].rearrange("p (t c) -> p t c", t=NT)
        adj_in = arena_a[:, NT * XW:].bitcast(I32).rearrange("p (s c) -> p s c", s=SLOTS)
        a01 = arena_b[:, 0:SLOTS * CJ * GI // 2].bitcast(BF16).rearrange("p (s c) -> p s c", s=SLOTS)
        node = arena_c[:, 0:512]
        node_t = arena_c[:, 512:1024]
        x_res = arena_c[:, 1024:1536]
        wh = arena_c[:, 1536:1536 + IT * HW].rearrange("p (t c) -> p t c", t=IT)
        v_new = arena_c[:, 2056:2056 + IT * VW].bitcast(F16).rearrange("p (t k c) -> p t k c", t=IT, k=2)
        x_all = mask[:, NG - 1, :].bitcast(F32).rearrange("p (t c) -> p t c", t=NT)
        x_rest = mask[:, NG - 2, :].bitcast(F32).rearrange("p (t c) -> p t c", t=NT)
        v_all = arena_a[:, 0:NT * 2 * VW].bitcast(F16).rearrange("p (t k c) -> p t k c", t=NT, k=2)
        neg_sum = arena_a[:, NT * 2 * VW:NT * 2 * VW + 2 * IT * VW].bitcast(F32).rearrange(
            "p (t c) -> p t c", t=IT)
        sign = arena_b[:, 0:RING * GW].rearrange("p (s c) -> p s c", s=RING)
        n_pos = arena_b[:, RING * GW:2 * RING * GW].rearrange("p (s c) -> p s c", s=RING)
        n_neg = arena_b[:, 2 * RING * GW:3 * RING * GW].rearrange("p (s c) -> p s c", s=RING)
        x1_back = arena_c[:, 0:512]
        pos_sum = arena_c[:, 512:512 + IT * VW].rearrange("p (t c) -> p t c", t=IT)
        joined = arena_c[:, 1544:1544 + IT * HW].rearrange("p (t c) -> p t c", t=IT)
        h_exp = arena_c[:, 1544:1544 + 512]
        h = arena_c[:, 2060:2572]
        h_min = arena_c[:, 2572:3084]
        last_exp = arena_b[:, 0:512].bitcast(F32)

        wide_wh = arena_a[:, 0:NT * HW * 2].bitcast(F32).rearrange("p (t c) -> p t c", t=NT)
        wide_total = arena_a[:, NT * HW * 2:(NT + IT) * HW * 2].bitcast(F32).rearrange("p (t c) -> p t c", t=IT)
        wide_b = arena_b.rearrange("p (k c) -> p k c", k=6).bitcast(F32)
        wide_sum, wide_prob, wide_is, wide_cand, wide_best, wide_max = (wide_b[:, k, :] for k in range(6))

        not_pos = sb("not_pos", [P, 2, GW], I32)
        f1_rows = sb("f1_rows", [P, 2 * GI], F32)
        ident = sb("ident", [P, P], F32)
        w0t_sb = sb("w0t_sb", [P, F], F32)
        w1_sb = sb("w1_sb", [P, F + 2], F32)
        w1t_sb = f1_rows[:, 0:F]
        v_first = sb("v_first", [P, IT, 2, VW], F16)
        a_sb = sb("a_sb", [P, 2], F32)
        b_rows = sb("b_rows", [P, F], F32)
        w_lim = sb("w_lim", [P, 4], F32)
        w_pow = sb("w_pow", [P, 1], F32)
        w_inv = sb("w_inv", [P, 1], F32)
        half = sb("half", [P, 1], F32)
        minus_half = sb("minus_half", [P, IT], F32)
        eps_cols = sb("eps_cols", [P, IT], F32)
        rdeg = sb("rdeg", [P, IT], F32)
        stats = sb("stats", [P, IT, 6], F32)
        moments = sb("moments", [P, IT, 2], F32)
        vare = sb("vare", [P, IT], F32)
        rstd = sb("rstd", [P, IT], F32)
        rden = sb("rden", [P, IT], F32)
        f_cols = sb("f_cols", [P, NT, 2], F32)
        thr = sb("thr", [P, NT], F32)
        weight = sb("weight", [P, IT, 2], F32)
        w_exp = sb("w_exp", [P, 2, IT, 2], I32)
        w_unit = sb("w_unit", [P, 2, IT, 2], I32)
        mant = sb("mant", [P, IT, 2], F32)
        power = sb("power", [P, NT * 2, 4], I8)
        f2_held = sb("f2_held", [P, IT], F32)
        f1_held = sb("f1_held", [P, NT], F32)
        row_arg = sb("row_arg", [P, 2, NT], F32)
        row_fac = sb("row_fac", [P, 2, NT], F32)
        f1_cols = sb("f1_cols", [P, IT], F32)
        f1_out = sb("f1_out", [IT, P], F32)
        f_lim = sb("f_lim", [P, 8], F32)
        is_wide = sb("is_wide", [P, 1], I32)

        acc = ctx.enter_context(nc.psum_tensor("acc", [P, 8, 512], F32))
        sums = acc[:, 0:IT, :]
        agg_t_ps = acc[:, 4, :]
        lin_ps = acc[:, 5, :]
        x1_t_ps = acc[:, 6, :]
        wh_ps = acc[:, 6:8, 0:2 * (F + 2)].rearrange("p b (t c) -> p b t c", t=2)
        f1_ps = acc[0:IT, 4, 0:P]
        wa_ps = acc[:, 7, 3 * P:3 * P + 2]

        last_agg_t_ps = acc[:, 0:IT, 0:P]
        last_lin_ps = acc[:, 0:IT, P:P + F]
        last_x1_t_ps = acc[:, 0:IT, 2 * P:3 * P]
        last_wh_ps = acc[:, IT:2 * IT, 0:F + 2]
        last_f1_ps = acc[0:IT, 2 * IT - 1, 2 * P:3 * P]
        wide_turned_ps = acc[:, 0, :]
        wide_wh_ps = acc[:, 1, :]
        wide_part = acc[:, 4:8, 0:HW]

        held_vector, held_pool, held_pe, held_sp = (sem("held_vector"), sem("held_pool"), sem("held_pe"),
                                                    sem("held_sp"))
        w_landed = sem("w_landed")
        XQ = 4
        x_landed = [sem(f"x_landed{i}") for i in range(XQ)]
        adj_landed = [sem(f"adj_landed{i}") for i in range(SLOTS)]
        xb_step = sem("xb_step")
        ident_ready = sem("ident_ready")
        consts_ready = sem("consts_ready")
        w_max_ready = sem("w_max_ready")
        w_all_ready = sem("w_all_ready")
        w_step = sem("w_step")
        wa_ready = sem("wa_ready")
        weights_ready = sem("weights_ready")
        x_hi_ready = sem("x_hi_ready")
        x_rest_ready = sem("x_rest_ready")
        x_mid_ready = sem("x_mid_ready")
        x_parts_ready = sem("x_parts_ready")
        a01_ready = sem("a01_ready")
        mask_ready = sem("mask_ready")
        chunk_used = sem("chunk_used")
        sums_ready = sem("sums_ready")
        sums_read = sem("sums_read")
        agg_t_ready = sem("agg_t_ready")
        agg_t_copied = sem("agg_t_copied")
        lin_ready = sem("lin_ready")
        xb_ready = sem("xb_ready")
        y_ready = sem("y_ready")
        stats_ready = sem("stats_ready")
        moments_ready = sem("moments_ready")
        pool_step = sem("pool_step")
        rstd_ready = sem("rstd_ready")
        x1_ready = sem("x1_ready")
        x1_stored = sem("x1_stored")
        x1_t_ready = sem("x1_t_ready")
        x1_t_copied = sem("x1_t_copied")
        wh_ready = sem("wh_ready")
        f1_ready = sem("f1_ready")
        f_copied = sem("f_copied")
        f2_held_ready = sem("f2_held_ready")
        f1_held_ready = sem("f1_held_ready")
        wh_copied = sem("wh_copied")
        f1_copied = sem("f1_copied")
        f1_stored = sem("f1_stored")
        weight_ready = sem("weight_ready")
        w_bits = sem("w_bits")
        mant_ready = sem("mant_ready")
        v_hi_ready = sem("v_hi_ready")
        v_lo_ready = sem("v_lo_ready")
        v_stored = sem("v_stored")
        v_landed = [sem(f"v_landed{i}") for i in range(NG - 2)]
        f1_landed = [sem("f1_landed_even"), sem("f1_landed_odd")]
        row_arg_ready = sem("row_arg_ready")
        row_fac_ready = sem("row_fac_ready")
        sign_ready = sem("sign_ready")
        pos_ready = sem("pos_ready")
        not_pos_ready = sem("not_pos_ready")
        neg_ready = sem("neg_ready")
        tile_used = sem("tile_used")
        acc_ready = sem("acc_ready")
        pos_read = sem("pos_read")
        neg_read = sem("neg_read")
        row_step = sem("row_step")
        last_sum_ready = sem("last_sum_ready")
        last_joined = sem("last_joined")
        last_minus_min = sem("last_minus_min")
        last_res_ready = sem("last_res_ready")
        last_pool_step = sem("last_pool_step")
        last_x1_added = sem("last_x1_added")
        last_scaled = sem("last_scaled")
        last_exp_ready = sem("last_exp_ready")
        joined_ready = sem("joined_ready")
        inv_ready = sem("inv_ready")
        rden_ready = sem("rden_ready")
        h_ready = sem("h_ready")
        min_ready = sem("min_ready")
        exp_ready = sem("exp_ready")
        elu_ready = sem("elu_ready")
        x1_back_landed = sem("x1_back_landed")
        res_ready = sem("res_ready")
        stats2_ready = sem("stats2_ready")
        moments2_ready = sem("moments2_ready")
        rstd2_ready = sem("rstd2_ready")
        normed = sem("normed")
        out_landed = sem("out_landed")
        lim_step = sem("lim_step")
        lim_ready = sem("lim_ready")
        lim_all_ready = sem("lim_all_ready")
        wide_known = sem("wide_known")
        wide_x1_landed = sem("wide_x1_landed")
        wide_turned = sem("wide_turned")
        wide_turned_copied = sem("wide_turned_copied")
        wide_wh_made = sem("wide_wh_made")
        wide_wh_copied = sem("wide_wh_copied")
        wide_rows_landed = sem("wide_rows_landed")
        wide_step = sem("wide_step")
        wide_best_ready = sem("wide_best_ready")
        wide_max_ready = sem("wide_max_ready")
        wide_arg_ready = sem("wide_arg_ready")
        wide_exp_ready = sem("wide_exp_ready")
        wide_prob_ready = sem("wide_prob_ready")
        wide_part_ready = sem("wide_part_ready")
        wide_part_added = sem("wide_part_added")
        wide_min_ready = sem("wide_min_ready")
        wide_elu_ready = sem("wide_elu_ready")
        wide_moments_ready = sem("wide_moments_ready")
        wide_pool_step = sem("wide_pool_step")
        wide_rstd_ready = sem("wide_rstd_ready")
        wide_normed = sem("wide_normed")
        wide_out_landed = sem("wide_out_landed")

        block = ctx.enter_context(nc.Block())
        LAST = NG - 1
        OUT_ALL = 16 * (LAST + 2)

        def sums_done(eng, g, t):
            if t < IT - 1:
                eng.wait_ge(sums_ready, g * (IT - 1) + (t + 1))
            else:
                eng.wait_ge(chunk_used, g * NC + NC)

        def acc_done(eng, g, t):
            if t < IT - 1:
                eng.wait_ge(acc_ready, g * (IT - 1) + (t + 1))
            else:
                eng.wait_ge(tile_used, g * NT + NT)

        def rows(t):
            return slice(t * F, (t + 1) * F)

        def denominators(g):
            nc.vector.wait_ge(joined_ready, g + 1)
            nc.vector.reciprocal(rden[:], joined[:, :, F]).then_inc(inv_ready, 1)
            nc.vector.wait_ge(inv_ready, g + 1)
            nc.vector.tensor_scalar(rden[:], rden[:], w_pow[:], None, ALU.mult).then_inc(rden_ready, 1)

        def minima(g):
            nc.vector.wait_ge(h_ready, g + 1)
            nc.vector.tensor_scalar(h_min, h, 0.0, None, ALU.min).then_inc(min_ready, 1)

        def row_moments(g):
            nc.vector.wait_ge(res_ready, g + 1)
            for t in range(IT):
                nc.vector.bn_stats(stats[:, t, :], h[:, rows(t)]).then_inc(stats2_ready, 1)
            for t in range(IT):
                nc.vector.wait_ge(stats2_ready, g * IT + (t + 1))
                nc.vector.sem_inc(held_vector, 1)
                nc.vector.bn_aggr(moments[:, t, :], stats[:, t, :]).then_inc(moments2_ready, 1)

        @block.sync
        def _(sp):
            def load_chunk(g, c):
                s = c % SLOTS
                if not (isinstance(g, int) and c < SLOTS):
                    sp.wait_ge(a01_ready, g * NC + (c - SLOTS + 1))
                    sp.wait_ge(mask_ready, g * NC + (c - SLOTS + 1))
                sp.dma_start(adj_in[:, s, :],
                             adj_tiles[bass.ds(g, 1), :, c * CJ * GI:(c + 1) * CJ * GI].rearrange(
                                 "g p n -> (g p) n")).then_inc(adj_landed[s], 16)

            for c in range(NC):
                load_chunk(0, c)
            with sp.Fori(1, NG) as g:
                for c in range(NC):
                    load_chunk(g, c)

            def load_f1(g, odd):
                sp.dma_start(f1_rows[:, odd * GI:(odd + 1) * GI],
                             f1_dram[bass.ds(g, 1)].rearrange("g a n -> (g a) n").to_broadcast([P, GI])).then_inc(
                                 f1_landed[odd], 16)

            sp.wait_ge(f1_stored, 16 * 2)
            load_f1(0, 0)
            load_f1(1, 1)
            sp.wait_ge(chunk_used, NG * NC)
            sp.wait_ge(a01_ready, NG * NC)
            sp.wait_ge(mask_ready, NG * NC)
            sp.wait_ge(xb_ready, NG)
            sp.wait_ge(v_stored, 16 * (LAST - 1))
            for g in range(1, LAST):
                sp.dma_start(v_all[:, g * IT:(g + 1) * IT, :, :].rearrange("p t k c -> p (t k c)"),
                             v_dram[g - 1]).then_inc(v_landed[g - 1], 16)

            def group_dmas(g, odd, load):
                sp.wait_ge(res_ready, g)
                sp.dma_start(x1_back, x1_dram[bass.ds(g, 1)].rearrange("g p n -> (g p) n")).then_inc(
                    x1_back_landed, 16)
                sp.wait_ge(normed, g)
                sp.dma_start(out_tiles[:, bass.ds(g * IT - IT, IT), :].rearrange("p t c -> p (t c)"), h).then_inc(
                    out_landed, 16)
                if load:
                    sp.wait_ge(sign_ready, g * NT + NT)
                    load_f1(g + 2, odd)

            sp.wait_ge(x1_stored, 16 * NG)
            sp.wait_ge(f1_stored, 16 * NG)
            sp.wait_ge(wh_ready, NG * IT)
            sp.dma_start(x1_back, x1_dram[0]).then_inc(x1_back_landed, 16)
            sp.wait_ge(sign_ready, NT)
            load_f1(2, 0)
            group_dmas(1, 1, True)
            with sp.Fori(1, NG // 2 - 1) as k:
                group_dmas(k * 2, 0, True)
                group_dmas(k * 2 + 1, 1, True)
            group_dmas(NG - 2, 0, False)
            group_dmas(NG - 1, 1, False)
            for t in range(0, IT, 2):
                sp.wait_ge(normed, LAST + (t + 2))
                sp.dma_start(out_tiles[:, LAST * IT + t:LAST * IT + t + 2, :].rearrange("p t c -> p (t c)"),
                             h[:, t * F:(t + 2) * F]).then_inc(out_landed, 16)
            sp.wait_ge(out_landed, OUT_ALL)

            sp.wait_ge(wide_known, 1)
            with sp.If(sp.value_load(is_wide[0:1, 0:1], min_val=0, max_val=1) > 0):
                with sp.Fori(0, NG) as g:
                    sp.dma_start(x1_back, x1_dram[bass.ds(g, 1)].rearrange("g p n -> (g p) n")).then_inc(
                        wide_x1_landed, 16)
                    sp.wait_ge(wide_turned, g + 1)
                    sp.sem_inc(held_sp, 1)
                with sp.Fori(0, NG) as g:
                    sp.dma_start(f1_rows[:, 0:GI],
                                 f1_dram[bass.ds(g, 1)].rearrange("g a n -> (g a) n").to_broadcast(
                                     [P, GI])).then_inc(wide_rows_landed, 16)
                    sp.dma_start(x1_back, x1_dram[bass.ds(g, 1)].rearrange("g p n -> (g p) n")).then_inc(
                        wide_rows_landed, 16)
                    sp.wait_ge(wide_normed, g + 1)
                    sp.sem_inc(held_sp, 1)
                    sp.dma_start(out_tiles[:, bass.ds(g * IT, IT), :].rearrange("p t c -> p (t c)"), h).then_inc(
                        wide_out_landed, 16)
                    sp.wait_ge(wide_out_landed, g * 16 + 16)
                    sp.sem_inc(held_sp, 1)

        @block.gpsimd
        def _(pool):
            nc.gpsimd.memset(ident[:], 1.0).then_inc(ident_ready, 1)
            pool.wait_ge(ident_ready, 1)
            nc.gpsimd.affine_select(out=ident[:], in_=ident[:], compare_op=ALU.is_equal, fill=0.0, base=0,
                                    pattern=[[-1, P]], channel_multiplier=1).then_inc(ident_ready, 1)
            nc.gpsimd.memset(minus_half[:], -0.5).then_inc(consts_ready, 1)
            nc.gpsimd.memset(eps_cols[:], EPS).then_inc(consts_ready, 1)
            nc.gpsimd.memset(wh[:, :, F:HW], 1.0).then_inc(consts_ready, 1)
            for k in range(NG):
                t = slice(k * IT, (k + 1) * IT)
                pool.wait_ge(x_hi_ready, k + 1)
                nc.gpsimd.tensor_tensor(x_rest[:, t, :], x_all[:, t, :], xparts[:, t, 0:F],
                                        ALU.subtract).then_inc(x_rest_ready, 1)
                pool.wait_ge(x_mid_ready, k + 1)
                nc.gpsimd.tensor_tensor(xparts[:, t, 2 * F:3 * F], x_rest[:, t, :], xparts[:, t, F:2 * F],
                                        ALU.subtract).then_inc(x_parts_ready, 1)
            def residual_rows(g):
                part = [xparts[:, bass.ds(g * IT, IT), k * F:(k + 1) * F] for k in range(3)]
                res = x_res.rearrange("p (t c) -> p t c", t=IT)
                nc.gpsimd.tensor_tensor(res, part[0], part[1], ALU.add).then_inc(xb_step, 1)
                pool.wait_ge(xb_step, g * 2 + 1)
                nc.gpsimd.tensor_tensor(res, res, part[2], ALU.add).then_inc(xb_step, 1)
                pool.wait_ge(xb_step, g * 2 + 2)
                nc.gpsimd.tensor_tensor(res, res,
                                        b_rows[:].rearrange("p (t c) -> p t c", t=1).to_broadcast([P, IT, F]),
                                        ALU.add).then_inc(xb_ready, 1)

            def layer0_rows(g, store_v=True, last=False):
                if not isinstance(g, int) or g > 1:
                    pool.wait_ge(v_stored, g * 16 - 16)
                halves = 2 if last else 1
                for k in range(halves):
                    t = slice(k * IT // halves, (k + 1) * IT // halves)
                    pool.wait_ge(moments_ready, g * IT + t.stop)
                    nc.gpsimd.tensor_tensor(vare[:, t], moments[:, t, 1], eps_cols[:, t], ALU.add).then_inc(
                        pool_step, 1)
                    pool.wait_ge(pool_step, g + (k + 1))
                    nc.gpsimd.tensor_tensor(rstd[:, t], vare[:, t], minus_half[:, t], ALU.pow).then_inc(
                        rstd_ready, 1)
                if not last:
                    residual_rows(g + 1)
                pool.wait_ge(x1_ready, g * IT + IT)
                pool.dma_start(x1_dram[bass.ds(g, 1)].rearrange("g p n -> (g p) n"), node).then_inc(x1_stored, 16)
                pool.wait_ge(f1_copied, g + 1)
                pool.dma_start(f1_dram[bass.ds(g, 1)].rearrange("g a (t n) -> (g a t) n", t=IT), f1_out[:]).then_inc(
                    f1_stored, 16)
                if store_v:
                    pool.wait_ge(v_lo_ready, g * 2 * IT + 2 * IT)
                    pool.dma_start(v_dram[bass.ds(g - 1, 1)].rearrange("g p n -> (g p) n"),
                                   v_new.rearrange("p t k c -> p (t k c)")).then_inc(v_stored, 16)

            pool.wait_ge(w_landed, 16 * 5)
            pool.wait_ge(x_parts_ready, NG)
            residual_rows(0)
            pool.wait_ge(w_max_ready, 1)
            nc.gpsimd.partition_all_reduce(w_lim[:, 3:4], w_lim[:, 2:3], P, bass.bass_isa.ReduceOp.max).then_inc(
                w_all_ready, 1)

            layer0_rows(0, store_v=False)
            layer0_rows(1)
            with pool.Fori(2, LAST) as g:
                layer0_rows(g)
            layer0_rows(LAST, store_v=False, last=True)

            pool.wait_ge(lim_ready, 1)
            nc.gpsimd.partition_all_reduce(f_lim[:, 7:8], f_lim[:, 6:7], P, bass.bass_isa.ReduceOp.max).then_inc(
                lim_all_ready, 1)
            def finish_rows(g):
                steps = g * 4
                h_t = h.rearrange("p (t c) -> p t c", t=IT)
                pool.wait_ge(pos_read, g * IT + IT)
                pool.wait_ge(neg_read, g * IT + IT)
                nc.gpsimd.tensor_tensor(pos_sum, pos_sum, neg_sum, ALU.add).then_inc(row_step, 1)
                pool.wait_ge(row_step, steps + 1)
                nc.gpsimd.tensor_tensor(joined, pos_sum[:, :, 0:HW], pos_sum[:, :, HW:VW], ALU.add).then_inc(
                    joined_ready, 1)
                if not (isinstance(g, int) and g == 0):
                    pool.wait_ge(out_landed, g * 16)
                pool.wait_ge(rden_ready, g + 1)
                nc.gpsimd.tensor_tensor(h_t, joined[:, :, 0:F],
                                        rden[:].rearrange("p (t k) -> p t k", k=1).to_broadcast([P, IT, F]),
                                        ALU.mult).then_inc(h_ready, 1)
                pool.wait_ge(min_ready, g + 1)
                nc.gpsimd.tensor_tensor(h, h, h_min, ALU.subtract).then_inc(row_step, 1)
                pool.wait_ge(x1_back_landed, g * 16 + 16)
                pool.wait_ge(row_step, steps + 2)
                nc.gpsimd.tensor_tensor(h, h, x1_back, ALU.add).then_inc(row_step, 1)
                pool.wait_ge(exp_ready, g + 1)
                pool.wait_ge(row_step, steps + 3)
                nc.gpsimd.tensor_tensor(h, h, h_exp, ALU.add).then_inc(res_ready, 1)
                pool.wait_ge(moments2_ready, g * IT + IT)
                nc.gpsimd.tensor_tensor(vare[:], moments[:, :, 1], eps_cols[:], ALU.add).then_inc(pool_step, 1)
                pool.wait_ge(pool_step, g + (NG + 2))
                nc.gpsimd.tensor_tensor(rstd[:], vare[:], minus_half[:], ALU.pow).then_inc(rstd2_ready, 1)
                nc.gpsimd.tensor_tensor(h_t, h_t, moments[:, :, 0:1].to_broadcast([P, IT, F]),
                                        ALU.subtract).then_inc(row_step, 1)
                pool.wait_ge(rstd2_ready, g + 1)
                pool.wait_ge(row_step, steps + 4)
                nc.gpsimd.tensor_tensor(h_t, h_t, rstd[:].rearrange("p (t k) -> p t k", k=1).to_broadcast([P, IT, F]),
                                        ALU.mult).then_inc(normed, 1)

            finish_rows(0)
            with pool.Fori(1, LAST) as g:
                finish_rows(g)
            pool.wait_ge(x1_back_landed, NG * 16)
            for t in range(IT):
                pool.wait_ge(min_ready, LAST + (t + 1))
                nc.gpsimd.tensor_tensor(h[:, rows(t)], h[:, rows(t)], h_min[:, rows(t)], ALU.subtract).then_inc(
                    last_minus_min, 1)
                pool.wait_ge(last_minus_min, t + 1)
                nc.gpsimd.tensor_tensor(h[:, rows(t)], h[:, rows(t)], x1_back[:, rows(t)], ALU.add).then_inc(
                    last_x1_added, 1)
            for k in range(2):
                t = slice(k * IT // 2, (k + 1) * IT // 2)
                pool.wait_ge(moments2_ready, LAST * IT + t.stop)
                nc.gpsimd.tensor_tensor(vare[:, t], moments[:, t, 1], eps_cols[:, t], ALU.add).then_inc(
                    last_pool_step, 1)
                pool.wait_ge(last_pool_step, k + 1)
                nc.gpsimd.tensor_tensor(rstd[:, t], vare[:, t], minus_half[:, t], ALU.pow).then_inc(
                    rstd2_ready, 1)

            pool.wait_ge(wide_known, 1)
            with pool.If(pool.value_load(is_wide[0:1, 0:1], min_val=0, max_val=1) > 0):
                with pool.Fori(0, NG) as g:
                    pool.wait_ge(wide_best_ready, g + 1)
                    pool.sem_inc(held_pool, 1)
                    nc.gpsimd.partition_all_reduce(wide_max, wide_best, P, bass.bass_isa.ReduceOp.max).then_inc(
                        wide_max_ready, 1)
                    pool.wait_ge(wide_moments_ready, g + 1)
                    nc.gpsimd.tensor_tensor(vare[:], moments[:, :, 1], eps_cols[:], ALU.add).then_inc(
                        wide_pool_step, 1)
                    pool.wait_ge(wide_pool_step, g + 1)
                    nc.gpsimd.tensor_tensor(rstd[:], vare[:], minus_half[:], ALU.pow).then_inc(wide_rstd_ready, 1)

        @block.scalar
        def _(act):
            QX = NT // XQ
            for q in range(XQ):
                act.dma_start(x_all[:, q * QX:(q + 1) * QX, :], x_tiles[:, q * QX:(q + 1) * QX, :]).then_inc(
                    x_landed[q], 16)
            act.dma_start(w1_sb[:, 0:F], w1).then_inc(w_landed, 16)
            act.dma_start(w1t_sb, w1t).then_inc(w_landed, 16)
            act.dma_start(w0t_sb[:], w0t).then_inc(w_landed, 16)
            act.dma_start(a_sb[:], a_cols).then_inc(w_landed, 16)
            act.dma_start(b_rows[:], b0.to_broadcast([P, F])).then_inc(w_landed, 16)

            def keep_mask(g, c):
                act.wait_ge(adj_landed[c % SLOTS], g * 16 * LAPS + 16 * (c // SLOTS + 1))
                nc.scalar.activation(
                    mask[:, bass.ds(g, 1), c * CJ * GW:(c + 1) * CJ * GW].rearrange("p g n -> p (g n)").bitcast(I8),
                    adj_in[:, c % SLOTS, :], ACT.Sign, bias=half[:], scale=-1.0).then_inc(mask_ready, 1)

            def weights_of_nodes(g):
                act.wait_ge(f2_held_ready, g + 1)
                nc.scalar.activation(weight[:, :, 0], f2_held[:], ACT.Exp)
                nc.scalar.activation(weight[:, :, 1], f2_held[:], ACT.Exp, scale=ALPHA).then_inc(weight_ready, 1)

            def high_parts(g, t, v):
                if t == 0:
                    act.wait_ge(mant_ready, g + 1)
                    act.wait_ge(wh_copied, g * IT + IT)
                for k in range(2):
                    nc.scalar.activation(v[:, t, k, 0:HW], wh[:, t, :], ACT.Copy,
                                         scale=mant[:, t, k:k + 1]).then_inc(v_hi_ready, 1)

            act.wait_ge(consts_ready, 4)
            for c in range(NC):
                keep_mask(0, c)

            def group(g, v):
                for c in range(NC):
                    keep_mask(g, c)
                    if c == 11:
                        weights_of_nodes(g - 1)
                    if c >= 12:
                        high_parts(g - 1, c - 12, v)

            act.wait_ge(x_parts_ready, NG)
            group(1, v_first)
            with act.Fori(2, NG) as g:
                group(g, v_new)
            for t in range(IT):
                act.wait_ge(agg_t_ready, LAST * IT + (t + 1))
                nc.scalar.activation(node_t[:, t * P:(t + 1) * P], last_agg_t_ps[:, t, :], ACT.Copy).then_inc(
                    agg_t_copied, 1)

            def sign_tile(g, odd, jt):
                s = jt % RING
                if jt == 0 and isinstance(g, int):
                    act.wait_ge(f1_landed[odd], 16)
                elif jt == 0:
                    act.wait_ge(f1_landed[odd], (g - odd) * 8 + 16)
                if not (isinstance(g, int) and g == 0 and jt < RING):
                    act.wait_ge(pos_ready, g * NT + (jt - RING + 1))
                nc.scalar.activation(sign[:, s, :].bitcast(I8), f1_rows[:, odd * GI:(odd + 1) * GI], ACT.Sign,
                                     bias=thr[:, jt:jt + 1], scale=-1.0).then_inc(sign_ready, 1)

            for jt in range(EARLY):
                sign_tile(0, 0, jt)

            def last_f(t):
                act.wait_ge(wh_ready, LAST * IT + (t + 1))
                nc.scalar.activation(f1_cols[:, t:t + 1], last_wh_ps[:, t, F:F + 1], ACT.Copy)
                nc.scalar.activation(f_cols[:, LAST * IT + t, :], last_wh_ps[:, t, F:F + 2], ACT.Copy).then_inc(
                    f_copied, 1)
                nc.scalar.activation(wh[:, t, 0:F], last_wh_ps[:, t, 0:F], ACT.Copy).then_inc(wh_copied, 1)

            for t in range(IT):
                act.wait_ge(x1_t_ready, LAST * IT + (t + 1))
                nc.scalar.activation(node_t[:, t * P:(t + 1) * P], last_x1_t_ps[:, t, :], ACT.Copy).then_inc(
                    x1_t_copied, 1)
                if t > 0:
                    last_f(t - 1)
            last_f(IT - 1)
            act.wait_ge(f1_stored, LAST * 16)
            act.wait_ge(f1_ready, NG)
            nc.scalar.activation(f1_out[:], last_f1_ps, ACT.Copy).then_inc(f1_copied, 1)

            def read_positive(g, first=False):
                for t in range(IT):
                    acc_done(act, g, t)
                    if t == 0 and not first:
                        act.wait_ge(joined_ready, g)
                    nc.scalar.activation(pos_sum[:, t, :], acc[:, 2 * t, 0:VW], ACT.Copy,
                                         scale=row_fac[:, 0, bass.ds(g * IT + t, 1)]).then_inc(pos_read, 1)

            def elu_exp(g):
                act.wait_ge(min_ready, g + 1)
                nc.scalar.activation(h_exp, h_min, ACT.Exp).then_inc(elu_ready, 1)
                act.wait_ge(elu_ready, g + 1)
                nc.scalar.activation(h_exp, h_exp, ACT.Copy, bias=-1.0).then_inc(exp_ready, 1)

            def group1(g, odd, tail=True, first=False):
                for jt in range(0 if tail else EARLY, NT):
                    sign_tile(g, odd, jt)
                    if not tail and jt == 6:
                        weights_of_nodes(LAST)
                    if not tail and jt == 14:
                        act.wait_ge(row_arg_ready, 2)
                        nc.scalar.activation(row_fac[:], row_arg[:], ACT.Exp).then_inc(row_fac_ready, 1)
                    if not tail and 15 <= jt < 15 + IT:
                        high_parts(LAST, jt - 15, v_all[:, LAST * IT:NG * IT])
                    if tail and jt == 6:
                        read_positive(g - 1, first)
                    if tail and jt == 20:
                        elu_exp(g - 1)

            group1(0, 0, tail=False)
            act.wait_ge(row_fac_ready, 1)
            act.wait_ge(x1_stored, 16 * NG)
            group1(1, 1, first=True)
            with act.Fori(1, NG // 2) as k:
                group1(k * 2, 0)
                group1(k * 2 + 1, 1)
            read_positive(LAST)
            for t in range(IT):
                act.wait_ge(min_ready, LAST + (t + 1))
                nc.scalar.activation(last_exp[:, rows(t)], h_min[:, rows(t)], ACT.Exp).then_inc(last_exp_ready, 1)

            act.wait_ge(wide_known, 1)
            with act.If(act.value_load(is_wide[0:1, 0:1], min_val=0, max_val=1) > 0):
                with act.Fori(0, NG) as g:
                    with act.Fori(0, NT) as jt:
                        act.wait_ge(wide_arg_ready, g * NT + jt + 1)
                        nc.scalar.activation(wide_prob, wide_sum, ACT.Exp).then_inc(wide_exp_ready, 1)
                    act.wait_ge(wide_min_ready, g + 1)
                    nc.scalar.activation(h_exp, h_min, ACT.Exp).then_inc(wide_elu_ready, 1)

        @block.tensor
        def _(pe):
            def chunk(g, c, count=1):
                pe.wait_ge(a01_ready, g * NC + (c + count))
                if isinstance(g, int) and c % 2 == 0:
                    pe.wait_ge(x_parts_ready, c // 2 + 1)
                for t in range(IT):
                    if c == 0 and not isinstance(g, int):
                        pe.wait_ge(sums_read, g * IT + (t - IT + 1))
                    for jt in range(c * CJ, (c + count) * CJ):
                        i0 = (jt % CJ) * GI + t * P
                        mm = nc.tensor.matmul(sums[:, t, 0:XW], a01[:, jt // CJ % SLOTS, i0:i0 + P],
                                              xparts[:, jt, :], start=(jt == 0), stop=(jt == NT - 1))
                    if t == IT - 1:
                        mm.then_inc(chunk_used, count)
                    elif c + count == NC:
                        mm.then_inc(sums_ready, 1)

            def turn_sums(g):
                for t in range(IT):
                    pe.wait_ge(sums_read, g * IT + (t + 1))
                    nc.tensor.transpose(agg_t_ps[:, t * P:(t + 1) * P], node[:, rows(t)], ident[:]).then_inc(
                        agg_t_ready, 1)

            def linear(g):
                for t in range(IT):
                    pe.wait_ge(agg_t_copied, g * IT + (t + 1))
                    nc.tensor.matmul(lin_ps[:, rows(t)], node_t[:, t * P:(t + 1) * P], w0t_sb[:],
                                     start=True, stop=True).then_inc(lin_ready, 1)

            def turn_x1(g):
                for t in range(IT):
                    pe.wait_ge(x1_ready, g * IT + (t + 1))
                    nc.tensor.transpose(x1_t_ps[:, t * P:(t + 1) * P], node[:, rows(t)], ident[:]).then_inc(
                        x1_t_ready, 1)

            def project(g):
                pe.wait_ge(weights_ready, 1)
                pe.wait_ge(x1_t_copied, g * IT + IT)
                for t in range(IT):
                    nc.tensor.matmul(wh_ps[:, t // 2, t % 2, :], node_t[:, t * P:(t + 1) * P], w1_sb[:],
                                     start=True, stop=True).then_inc(wh_ready, 1)

            def turn_f1(g):
                pe.wait_ge(f_copied, g * IT + IT)
                nc.tensor.transpose(f1_ps, f1_cols[:], ident[:]).then_inc(f1_ready, 1)

            def last_rows():
                for t in range(IT):
                    pe.wait_ge(sums_read, LAST * IT + (t + 1))
                    nc.tensor.transpose(last_agg_t_ps[:, t, :], node[:, rows(t)], ident[:]).then_inc(agg_t_ready, 1)
                    if t > 0:
                        last_linear(t - 1)
                last_linear(IT - 1)
                for t in range(IT):
                    pe.wait_ge(x1_ready, LAST * IT + (t + 1))
                    nc.tensor.transpose(last_x1_t_ps[:, t, :], node[:, rows(t)], ident[:]).then_inc(x1_t_ready, 1)
                    if t > 0:
                        last_project(t - 1)
                last_project(IT - 1)

            def last_linear(t):
                pe.wait_ge(agg_t_copied, LAST * IT + (t + 1))
                nc.tensor.matmul(last_lin_ps[:, t, :], node_t[:, t * P:(t + 1) * P], w0t_sb[:],
                                 start=True, stop=True).then_inc(lin_ready, 1)

            def last_project(t):
                pe.wait_ge(x1_t_copied, LAST * IT + (t + 1))
                nc.tensor.matmul(last_wh_ps[:, t, :], node_t[:, t * P:(t + 1) * P], w1_sb[:],
                                 start=True, stop=True).then_inc(wh_ready, 1)

            pe.wait_ge(ident_ready, 2)
            for c in range(NC - 2):
                chunk(0, c)
                if c == NC // 2:
                    pe.wait_ge(w_landed, 16 * 5)
                    nc.tensor.matmul(wa_ps, w1t_sb, a_sb[:], start=True, stop=True).then_inc(wa_ready, 1)
            chunk(0, NC - 2, 2)
            with pe.Fori(1, NG) as g:
                for c in range(NC - 2):
                    chunk(g, c)
                    if c == 0:
                        turn_sums(g - 1)
                    if c == 2:
                        linear(g - 1)
                    if c == 6:
                        turn_x1(g - 1)
                    if c == 8:
                        project(g - 1)
                    if c == 11:
                        turn_f1(g - 1)
                chunk(g, NC - 2, 2)
            last_rows()

            def alone():
                pe.sem_inc(held_pe, 1)

            def tiles(g, first, count):
                if isinstance(g, int) and first % IT == 0:
                    if first < LAST * IT:
                        if first > 0:
                            pe.wait_ge(v_landed[first // IT - 1], 16)
                    else:
                        pe.wait_ge(v_lo_ready, NG * 2 * IT)
                pe.wait_ge(pos_ready, g * NT + (first + count))
                pe.wait_ge(neg_ready, g * NT + (first + count))
                alone()
                for t in range(IT):
                    if isinstance(g, int) and first == 0 and t == IT // 2:
                        pe.wait_ge(wh_copied, NG * IT)
                        nc.tensor.transpose(last_f1_ps, f1_cols[:], ident[:]).then_inc(f1_ready, 1)
                    if isinstance(g, int) and first == 0 and t == IT - 1:
                        pe.wait_ge(f1_copied, NG)
                    for k, (operand, read) in enumerate(((n_pos, pos_read), (n_neg, neg_read))):
                        if first == 0 and not isinstance(g, int):
                            pe.wait_ge(read, g * IT + (t + 1 - IT))
                            alone()
                        for jt in range(first, first + count):
                            mm = nc.tensor.matmul(acc[:, 2 * t + k, 0:VW],
                                                  operand[:, jt % RING, t * P // 4:(t + 1) * P // 4].bitcast(F8),
                                                  (v_first if jt < IT else v_all)[:, jt, k, :],
                                                  start=(jt == 0), stop=(jt == NT - 1))
                    if t == IT - 1:
                        mm.then_inc(tile_used, count)
                    elif first + count == NT:
                        mm.then_inc(acc_ready, 1)

            for first, count in ((0, 1), (1, 1)):
                tiles(0, first, count)
            for first in range(BLOCK, NT, BLOCK):
                tiles(0, first, BLOCK)
            with pe.Fori(1, NG) as g:
                for first in range(0, NT, BLOCK):
                    tiles(g, first, BLOCK)

            pe.wait_ge(wide_known, 1)
            with pe.If(pe.value_load(is_wide[0:1, 0:1], min_val=0, max_val=1) > 0):
                pe.wait_ge(out_landed, OUT_ALL)
                with pe.Fori(0, NG) as g:
                    pe.wait_ge(wide_x1_landed, g * 16 + 16)
                    alone()
                    for t in range(IT):
                        mm = nc.tensor.transpose(wide_turned_ps[:, t * P:(t + 1) * P], x1_back[:, rows(t)], ident[:])
                    mm.then_inc(wide_turned, 1)
                    pe.wait_ge(wide_turned_copied, g + 1)
                    alone()
                    for t in range(IT):
                        mm = nc.tensor.matmul(wide_wh_ps[:, rows(t)], h_min[:, t * P:(t + 1) * P], w1_sb[:, 0:F],
                                              start=True, stop=True)
                    mm.then_inc(wide_wh_made, 1)
                    pe.wait_ge(wide_wh_copied, g + 1)
                    alone()
                with pe.Fori(0, NG) as g:
                    with pe.Fori(0, NT) as jt:
                        pe.wait_ge(wide_prob_ready, g * NT + jt + 1)
                        alone()
                        for t in range(IT):
                            mm = nc.tensor.matmul(wide_part[:, t, :], wide_prob[:, t * P:(t + 1) * P],
                                                  wide_wh[:, bass.ds(jt, 1), :].rearrange("p t c -> p (t c)"),
                                                  start=True, stop=True)
                        mm.then_inc(wide_part_ready, 1)
                        pe.wait_ge(wide_part_added, g * NT + jt + 1)
                        alone()

        @block.vector
        def _(dve):
            def alone():
                dve.sem_inc(held_vector, 1)

            nc.vector.memset(half[:], 0.5).then_inc(consts_ready, 1)
            nc.vector.memset(xparts[:, :, 3 * F:XW], 1.0).then_inc(w_step, 1)

            def high_part(k):
                t = slice(k * IT, (k + 1) * IT)
                dve.wait_ge(x_landed[k * XQ // NG], 16)
                nc.vector.tensor_copy(xparts[:, t, 0:F], x_all[:, t, :]).then_inc(x_hi_ready, 1)

            def middle_part(k):
                t = slice(k * IT, (k + 1) * IT)
                dve.wait_ge(x_rest_ready, k + 1)
                nc.vector.tensor_copy(xparts[:, t, F:2 * F], x_rest[:, t, :]).then_inc(x_mid_ready, 1)

            def binarise(g, c):
                s = c % SLOTS
                dve.wait_ge(adj_landed[s], g * 16 * LAPS + 16 * (c // SLOTS + 1))
                if not (isinstance(g, int) and g == 0 and c < SLOTS):
                    dve.wait_ge(chunk_used, g * NC + (c - SLOTS + 1))
                nc.vector.tensor_scalar(a01[:, s, :], adj_in[:, s, :], 1.0, None, ALU.is_equal).then_inc(a01_ready, 1)

            high_part(0)
            high_part(1)
            for c in range(NC):
                if c % 2 == 0:
                    middle_part(c // 2)
                    if c // 2 + 2 < NG:
                        high_part(c // 2 + 2)
                binarise(0, c)

            def largest_weight():
                dve.wait_ge(w_landed, 16 * 5)
                nc.vector.tensor_reduce(w_lim[:, 0:1], w1_sb[:, 0:F], AX.X, ALU.max).then_inc(w_step, 1)
                nc.vector.tensor_reduce(w_lim[:, 1:2], w1_sb[:, 0:F], AX.X, ALU.min).then_inc(w_step, 1)
                dve.wait_ge(w_step, 3)
                nc.vector.scalar_tensor_tensor(w_lim[:, 2:3], w_lim[:, 1:2], -1.0, w_lim[:, 0:1], ALU.mult,
                                               ALU.max).then_inc(w_max_ready, 1)

            def scale_weights():
                dve.wait_ge(w_all_ready, 1)
                nc.vector.tensor_scalar(w_lim[:, 2:3], w_lim[:, 3:4], 1e-30, 1e37, ALU.max, ALU.min).then_inc(
                    w_step, 1)
                dve.wait_ge(w_step, 4)
                nc.vector.tensor_scalar(w_pow[:].bitcast(I32), w_lim[:, 2:3].bitcast(I32), EXP_BITS, None,
                                        ALU.bitwise_and).then_inc(w_step, 1)
                dve.wait_ge(w_step, 5)
                nc.vector.reciprocal(w_inv[:], w_pow[:]).then_inc(w_step, 1)
                dve.wait_ge(w_step, 6)
                nc.vector.tensor_scalar(w1_sb[:, 0:F], w1_sb[:, 0:F], w_inv[:], None, ALU.mult)
                dve.wait_ge(wa_ready, 1)
                nc.vector.tensor_copy(w1_sb[:, F:F + 2], wa_ps).then_inc(weights_ready, 1)

            def read_sums(g, first=False):
                if not first:
                    dve.wait_ge(x1_stored, g * 16)
                for t in range(IT):
                    sums_done(dve, g, t)
                    nc.vector.tensor_reduce(node[:, rows(t)],
                                            sums[:, t, 0:3 * F].rearrange("p (k f) -> p f k", k=3),
                                            AX.X, ALU.add)
                    nc.vector.reciprocal(rdeg[:, t:t + 1], sums[:, t, 3 * F:XW]).then_inc(sums_read, 1)

            def copy_turned(dst, src, ready, done, g):
                dve.wait_ge(ready, g * IT + IT)
                nc.vector.tensor_copy(dst, src).then_inc(done, IT)

            def residual(g):
                dve.wait_ge(xb_ready, g + 1)
                dve.wait_ge(lin_ready, g * IT + IT)
                for t in range(IT):
                    nc.vector.scalar_tensor_tensor(node[:, rows(t)], lin_ps[:, rows(t)], rdeg[:, t:t + 1],
                                                   x_res[:, rows(t)], ALU.mult, ALU.add).then_inc(y_ready, 1)

            def y_moments(g):
                for t in range(IT):
                    dve.wait_ge(y_ready, g * IT + (t + 1))
                    nc.vector.bn_stats(stats[:, t, :], node[:, rows(t)]).then_inc(stats_ready, 1)
                for t in range(IT):
                    dve.wait_ge(stats_ready, g * IT + (t + 1))
                    alone()
                    nc.vector.bn_aggr(moments[:, t, :], stats[:, t, :]).then_inc(moments_ready, 1)

            def normalise(g):
                dve.wait_ge(rstd_ready, g + 1)
                for t in range(IT):
                    nc.vector.tensor_scalar(node[:, rows(t)], node[:, rows(t)], moments[:, t, 0:1],
                                            rstd[:, t:t + 1], ALU.subtract, ALU.mult).then_inc(x1_ready, 1)

            def take_f(g):
                dve.wait_ge(wh_ready, g * IT + IT)
                fc = f_cols[:, bass.ds(g * IT, IT), :]
                nc.vector.tensor_copy(f1_cols[:].rearrange("p (b t c) -> p b t c", b=2, c=1),
                                      wh_ps[:, :, :, F:F + 1])
                nc.vector.tensor_copy(fc.rearrange("p (b t) c -> p b t c", b=2), wh_ps[:, :, :, F:F + 2]).then_inc(
                    f_copied, IT)
                nc.vector.tensor_copy(wh[:, :, 0:F].rearrange("p (b t) c -> p b t c", b=2),
                                      wh_ps[:, :, :, 0:F]).then_inc(wh_copied, IT)
                hold_f2(g)

            def hold_f2(g):
                dve.wait_ge(f_copied, g * IT + IT)
                nc.vector.tensor_scalar(f2_held[:], f_cols[:, bass.ds(g * IT, IT), 1:2].rearrange("p t k -> p (t k)"),
                                        -F2_HELD, F2_HELD, ALU.max, ALU.min).then_inc(f2_held_ready, 1)

            def take_f1(g, first=False):
                if not first:
                    dve.wait_ge(f1_stored, g * 16)
                dve.wait_ge(f1_ready, g + 1)
                nc.vector.tensor_copy(f1_out[:], f1_ps).then_inc(f1_copied, 1)

            def split_weights(g):
                dve.wait_ge(f_copied, g * IT + IT)
                nc.vector.tensor_scalar(thr[:, bass.ds(g * IT, IT)],
                                        f_cols[:, bass.ds(g * IT, IT), 1:2].rearrange("p t k -> p (t k)"),
                                        -1.0, None, ALU.mult)
                base = g * 4
                dve.wait_ge(weight_ready, g + 1)
                nc.vector.tensor_scalar(w_exp[:, 0], weight[:].bitcast(I32), 23, None,
                                        ALU.logical_shift_right).then_inc(w_bits, 1)
                dve.wait_ge(w_bits, base + 1)
                nc.vector.tensor_scalar(w_exp[:, 1], w_exp[:, 0], float(F8_LOW), float(F8_HIGH), ALU.max,
                                        ALU.min).then_inc(w_bits, 1)
                dve.wait_ge(w_bits, base + 2)
                nc.vector.tensor_scalar(w_unit[:, 0], w_exp[:, 1], -1.0, float(2 * F32_BIAS + MANT_SHIFT), ALU.mult,
                                        ALU.add).then_inc(w_bits, 1)
                nc.vector.tensor_scalar(
                    power[:, bass.ds(g * IT * 2, IT * 2), :],
                    w_exp[:, 1].rearrange("p t (k o) -> p (t k) o", o=1).to_broadcast([P, IT * 2, 4]),
                    float(F8_BIAS - F32_BIAS), 4.0, ALU.add, ALU.mult)
                dve.wait_ge(w_bits, base + 3)
                nc.vector.tensor_scalar(w_unit[:, 1], w_unit[:, 0], 23, None,
                                        ALU.logical_shift_left).then_inc(w_bits, 1)
                dve.wait_ge(w_bits, base + 4)
                nc.vector.tensor_tensor(mant[:], weight[:], w_unit[:, 1].bitcast(F32), ALU.mult).then_inc(
                    mant_ready, 1)

            def low_parts(g, t, v):
                for k in range(2):
                    dve.wait_ge(v_hi_ready, g * 2 * IT + (2 * t + k + 1))
                    nc.vector.scalar_tensor_tensor(v[:, t, k, HW:VW], wh[:, t, :], mant[:, t, k:k + 1],
                                                   v[:, t, k, 0:HW], ALU.mult, ALU.subtract).then_inc(v_lo_ready, 1)

            def group(g, v, first=False):
                m = g - 1
                for c in range(NC):
                    binarise(g, c)
                    if first and c == 1:
                        largest_weight()
                    if first and c == 5:
                        scale_weights()
                    if c == 0:
                        read_sums(m, first)
                    if c == 2:
                        copy_turned(node_t, agg_t_ps, agg_t_ready, agg_t_copied, m)
                    if c == 4:
                        residual(m)
                    if c == 5:
                        y_moments(m)
                    if c == 7:
                        normalise(m)
                    if c == 8:
                        copy_turned(node_t, x1_t_ps, x1_t_ready, x1_t_copied, m)
                    if c == 10:
                        take_f(m)
                    if c == 11:
                        split_weights(m)
                    if c == 12:
                        take_f1(m, first)
                    if c >= 14:
                        low_parts(m, c - 14, v)
                low_parts(m, 2, v)
                low_parts(m, 3, v)

            group(1, v_first, True)
            with dve.Fori(2, NG) as g:
                group(g, v_new)

            def last_read(t):
                sums_done(dve, LAST, t)
                nc.vector.tensor_reduce(node[:, rows(t)], sums[:, t, 0:3 * F].rearrange("p (k f) -> p f k", k=3),
                                        AX.X, ALU.add)
                nc.vector.reciprocal(rdeg[:, t:t + 1], sums[:, t, 3 * F:XW]).then_inc(sums_read, 1)

            def last_residual(t):
                dve.wait_ge(lin_ready, LAST * IT + (t + 1))
                nc.vector.scalar_tensor_tensor(node[:, rows(t)], last_lin_ps[:, t, :], rdeg[:, t:t + 1],
                                               x_res[:, rows(t)], ALU.mult, ALU.add).then_inc(y_ready, 1)
                dve.wait_ge(y_ready, LAST * IT + (t + 1))
                nc.vector.bn_stats(stats[:, t, :], node[:, rows(t)]).then_inc(stats_ready, 1)
                dve.wait_ge(stats_ready, LAST * IT + (t + 1))
                nc.vector.bn_aggr(moments[:, t, :], stats[:, t, :]).then_inc(moments_ready, 1)

            def last_normalise(t):
                dve.wait_ge(rstd_ready, LAST + (t // 2 + 1))
                nc.vector.tensor_scalar(node[:, rows(t)], node[:, rows(t)], moments[:, t, 0:1],
                                        rstd[:, t:t + 1], ALU.subtract, ALU.mult).then_inc(x1_ready, 1)

            dve.wait_ge(x1_stored, LAST * 16)
            last_read(0)
            last_read(1)
            last_read(2)
            dve.wait_ge(xb_ready, NG)
            last_residual(0)
            last_read(3)
            last_residual(1)
            last_residual(2)
            last_residual(3)
            for t in range(IT):
                last_normalise(t)

            def find_limits():
                for k in range(2):
                    f = f_cols[:, :, k]
                    nc.vector.tensor_reduce(f_lim[:, 3 * k:3 * k + 1], f, AX.X, ALU.max).then_inc(lim_step, 1)
                    nc.vector.tensor_reduce(f_lim[:, 3 * k + 1:3 * k + 2], f, AX.X, ALU.min).then_inc(lim_step, 1)
                dve.wait_ge(lim_step, 4)
                for k in range(2):
                    nc.vector.scalar_tensor_tensor(f_lim[:, 3 * k + 2:3 * k + 3], f_lim[:, 3 * k + 1:3 * k + 2],
                                                   -1.0, f_lim[:, 3 * k:3 * k + 1], ALU.mult, ALU.max).then_inc(
                                                       lim_step, 1)
                dve.wait_ge(lim_step, 6)
                nc.vector.scalar_tensor_tensor(f_lim[:, 6:7], f_lim[:, 2:3], F2_LIMIT / F1_LIMIT, f_lim[:, 5:6],
                                               ALU.mult, ALU.max).then_inc(lim_ready, 1)

            def factor_arguments():
                nc.vector.tensor_scalar(f1_held[:], f_cols[:, :, 0], -F1_HELD, F1_HELD, ALU.max, ALU.min).then_inc(
                    f1_held_ready, 1)
                dve.wait_ge(f1_held_ready, 1)
                nc.vector.tensor_scalar(row_arg[:, 0, :], f1_held[:], 0.0, 1.0 - ALPHA, ALU.min,
                                        ALU.mult).then_inc(row_arg_ready, 1)
                nc.vector.tensor_scalar(row_arg[:, 1, :], f1_held[:], 0.0, ALPHA - 1.0, ALU.max,
                                        ALU.mult).then_inc(row_arg_ready, 1)

            def pattern(jt, k):
                return power[:, 2 * jt + k, :].bitcast(I32)

            def masks(g, jt):
                return mask[:, bass.ds(g, 1), jt * GW:(jt + 1) * GW].rearrange("p g n -> p (g n)")

            def positive_tile(g, jt):
                if not (isinstance(g, int) and g == 0 and jt < RING):
                    dve.wait_ge(tile_used, g * NT + (jt - RING + 1))
                nc.vector.scalar_tensor_tensor(n_pos[:, jt % RING, :], sign[:, jt % RING, :], pattern(jt, 0),
                                               masks(g, jt), ALU.bitwise_and, ALU.bitwise_and).then_inc(
                                                   pos_ready, 1)

            def not_positive_tile(g, jt):
                dve.wait_ge(sign_ready, g * NT + (jt + 1))
                nc.vector.scalar_tensor_tensor(not_pos[:, jt % 2, :], sign[:, jt % RING, :], -1, masks(g, jt),
                                               ALU.bitwise_xor, ALU.bitwise_and).then_inc(not_pos_ready, 1)

            def negative_tile(g, jt):
                dve.wait_ge(not_pos_ready, g * NT + (jt + 1))
                nc.vector.tensor_scalar(n_neg[:, jt % RING, :], not_pos[:, jt % 2, :], pattern(jt, 1), None,
                                        ALU.bitwise_and).then_inc(neg_ready, 1)

            def read_negative(g, first=False):
                for t in range(IT):
                    acc_done(dve, g, t)
                    if t == 0 and not first:
                        dve.wait_ge(joined_ready, g)
                    nc.vector.tensor_scalar(neg_sum[:, t, :], acc[:, 2 * t + 1, 0:VW],
                                            row_fac[:, 1, bass.ds(g * IT + t, 1)], None, ALU.mult).then_inc(
                                                neg_read, 1)

            def group1(g, tail=True, first=False):
                for jt in range(NT):
                    not_positive_tile(g, jt)
                    positive_tile(g, jt)
                    negative_tile(g, jt)
                    if not tail and jt == 2:
                        hold_f2(LAST)
                    if not tail and jt == 4:
                        split_weights(LAST)
                    if not tail and jt == 6:
                        factor_arguments()
                    if not tail and jt == 8:
                        find_limits()
                    if not tail and 13 <= jt < 13 + IT:
                        low_parts(LAST, jt - 13, v_all[:, LAST * IT:NG * IT])
                    if tail and jt == 5:
                        read_negative(g - 1, first)
                    if tail and jt == 11:
                        denominators(g - 1)
                    if tail and jt == 14:
                        minima(g - 1)
                    if tail and jt == 22:
                        row_moments(g - 1)

            def wide_rows():
                dve.wait_ge(out_landed, OUT_ALL)
                nc.vector.memset(wide_wh[:, :, F:HW], 1.0)
                with dve.Fori(0, NG) as g:
                    dve.wait_ge(wide_turned, g + 1)
                    nc.vector.tensor_copy(h_min, wide_turned_ps).then_inc(wide_turned_copied, 1)
                    dve.wait_ge(wide_wh_made, g + 1)
                    nc.vector.tensor_copy(wide_wh[:, bass.ds(g * IT, IT), 0:F],
                                          wide_wh_ps.rearrange("p (t c) -> p t c", t=IT)).then_inc(wide_wh_copied, 1)

                FIND, SUM, END = 4, 5, 10
                STEPS = 2 + NT * FIND + 2 + NT * SUM + END

                def is_neighbour(g, jt):
                    return nc.vector.tensor_scalar(
                        wide_is, mask[:, bass.ds(g, 1), bass.ds(jt * GW, GW)].rearrange("p g n -> p (g n)").bitcast(I8),
                        0.0, -1.0, ALU.min, ALU.mult)

                def f2_col(jt):
                    return f_cols[:, bass.ds(jt, 1), 1:2].rearrange("p t k -> p (t k)")

                with dve.Fori(0, NG) as g:
                    n = g * STEPS
                    nc.vector.memset(wide_best, -WIDE).then_inc(wide_step, 1)
                    nc.vector.memset(wide_total, 0.0).then_inc(wide_step, 1)
                    n = n + 2
                    with dve.Fori(0, NT) as jt:
                        m = n + jt * FIND
                        dve.wait_ge(wide_step, m)
                        is_neighbour(g, jt).then_inc(wide_step, 1)
                        dve.wait_ge(wide_step, m + 1)
                        nc.vector.tensor_scalar(wide_cand, wide_is, -1.0, WIDE, ALU.add, ALU.mult).then_inc(
                            wide_step, 1)
                        dve.wait_ge(wide_step, m + 2)
                        nc.vector.scalar_tensor_tensor(wide_cand, wide_is, f2_col(jt), wide_cand, ALU.mult,
                                                       ALU.add).then_inc(wide_step, 1)
                        dve.wait_ge(wide_step, m + 3)
                        nc.vector.tensor_tensor(wide_best, wide_best, wide_cand, ALU.max).then_inc(wide_step, 1)
                    n = n + NT * FIND
                    dve.wait_ge(wide_step, n)
                    dve.sem_inc(wide_best_ready, 1)
                    dve.wait_ge(wide_rows_landed, g * 32 + 32)
                    dve.wait_ge(wide_max_ready, g + 1)
                    nc.vector.tensor_tensor(wide_max, wide_max, f1_rows[:, 0:GI], ALU.add).then_inc(wide_step, 1)
                    dve.wait_ge(wide_step, n + 1)
                    nc.vector.scalar_tensor_tensor(wide_max, wide_max, ALPHA, wide_max, ALU.mult,
                                                   ALU.max).then_inc(wide_step, 1)
                    n = n + 2
                    with dve.Fori(0, NT) as jt:
                        m = n + jt * SUM
                        dve.wait_ge(wide_step, m)
                        is_neighbour(g, jt)
                        nc.vector.tensor_scalar(wide_sum, f1_rows[:, 0:GI], f2_col(jt), None, ALU.add).then_inc(
                            wide_step, 1)
                        dve.wait_ge(wide_step, m + 1)
                        nc.vector.scalar_tensor_tensor(wide_sum, wide_sum, ALPHA, wide_sum, ALU.mult,
                                                       ALU.max).then_inc(wide_step, 1)
                        dve.wait_ge(wide_step, m + 2)
                        nc.vector.tensor_tensor(wide_sum, wide_sum, wide_max, ALU.subtract).then_inc(wide_step, 1)
                        dve.wait_ge(wide_step, m + 3)
                        nc.vector.tensor_scalar(wide_sum, wide_sum, 0.0, None, ALU.min).then_inc(wide_arg_ready, 1)
                        dve.wait_ge(wide_exp_ready, g * NT + jt + 1)
                        nc.vector.tensor_tensor(wide_prob, wide_prob, wide_is, ALU.mult).then_inc(wide_prob_ready, 1)
                        dve.wait_ge(wide_part_ready, g * NT + jt + 1)
                        nc.vector.tensor_tensor(wide_total, wide_total, wide_part, ALU.add).then_inc(
                            wide_part_added, 1)
                        dve.wait_ge(wide_part_added, g * NT + jt + 1)
                        dve.sem_inc(wide_step, 2)
                    n = n + NT * SUM
                    rows3 = h.rearrange("p (t c) -> p t c", t=IT)
                    dve.wait_ge(wide_step, n)
                    nc.vector.reciprocal(rden[:], wide_total[:, :, F]).then_inc(wide_step, 1)
                    dve.wait_ge(wide_step, n + 1)
                    nc.vector.tensor_scalar(rden[:], rden[:], w_pow[:], None, ALU.mult).then_inc(wide_step, 1)
                    dve.wait_ge(wide_step, n + 2)
                    nc.vector.tensor_tensor(rows3, wide_total[:, :, 0:F],
                                            rden[:].rearrange("p (t k) -> p t k", k=1).to_broadcast([P, IT, F]),
                                            ALU.mult).then_inc(wide_step, 1)
                    dve.wait_ge(wide_step, n + 3)
                    nc.vector.tensor_scalar(h_min, h, 0.0, None, ALU.min).then_inc(wide_min_ready, 1)
                    dve.wait_ge(wide_elu_ready, g + 1)
                    nc.vector.tensor_scalar(h_exp, h_exp, -1.0, None, ALU.add).then_inc(wide_step, 1)
                    nc.vector.tensor_tensor(h, h, h_min, ALU.subtract).then_inc(wide_step, 1)
                    dve.wait_ge(wide_step, n + 5)
                    nc.vector.tensor_tensor(h, h, x1_back, ALU.add).then_inc(wide_step, 1)
                    dve.wait_ge(wide_step, n + 6)
                    nc.vector.tensor_tensor(h, h, h_exp, ALU.add).then_inc(wide_step, 1)
                    dve.wait_ge(wide_step, n + 7)
                    alone()
                    for t in range(IT):
                        b = nc.vector.bn_stats(stats[:, t, :], h[:, rows(t)])
                    b.then_inc(wide_step, 1)
                    dve.wait_ge(wide_step, n + 8)
                    alone()
                    for t in range(IT):
                        b = nc.vector.bn_aggr(moments[:, t, :], stats[:, t, :])
                    b.then_inc(wide_moments_ready, 1)
                    dve.wait_ge(wide_moments_ready, g + 1)
                    nc.vector.tensor_tensor(rows3, rows3, moments[:, :, 0:1].to_broadcast([P, IT, F]),
                                            ALU.subtract).then_inc(wide_step, 1)
                    dve.wait_ge(wide_rstd_ready, g + 1)
                    dve.wait_ge(wide_step, n + 9)
                    nc.vector.tensor_tensor(rows3, rows3,
                                            rstd[:].rearrange("p (t k) -> p t k", k=1).to_broadcast([P, IT, F]),
                                            ALU.mult).then_inc(wide_normed, 1)
                    dve.wait_ge(wide_normed, g + 1)
                    dve.sem_inc(wide_step, 1)

            group1(0, tail=False)
            dve.wait_ge(row_fac_ready, 1)
            group1(1, first=True)
            dve.wait_ge(lim_all_ready, 1)
            nc.vector.tensor_scalar(is_wide[:], f_lim[:, 7:8], F2_LIMIT, None, ALU.is_gt).then_inc(wide_known, 1)
            with dve.Fori(2, NG) as g:
                group1(g)

            def last_rows_of(pair):
                for t in pair:
                    acc_done(dve, LAST, t)
                    if t == 0:
                        dve.wait_ge(joined_ready, LAST)
                    dve.wait_ge(pos_read, LAST * IT + (t + 1))
                    nc.vector.scalar_tensor_tensor(neg_sum[:, t, :], acc[:, 2 * t + 1, 0:VW],
                                                   row_fac[:, 1, LAST * IT + t:LAST * IT + t + 1], pos_sum[:, t, :],
                                                   ALU.mult, ALU.add).then_inc(last_sum_ready, 1)
                    if t == 0:
                        dve.wait_ge(out_landed, LAST * 16)
                for t in pair:
                    dve.wait_ge(last_sum_ready, t + 1)
                    nc.vector.tensor_tensor(joined[:, t, :], neg_sum[:, t, 0:HW], neg_sum[:, t, HW:VW],
                                            ALU.add).then_inc(last_joined, 1)
                for t in pair:
                    dve.wait_ge(last_joined, t + 1)
                    nc.vector.reciprocal(rden[:, t:t + 1], joined[:, t, F:HW]).then_inc(inv_ready, 1)
                for t in pair:
                    dve.wait_ge(inv_ready, LAST + (t + 1))
                    nc.vector.tensor_scalar(h[:, rows(t)], joined[:, t, 0:F], rden[:, t:t + 1], w_pow[:], ALU.mult,
                                            ALU.mult).then_inc(last_scaled, 1)
                for t in pair:
                    dve.wait_ge(last_scaled, t + 1)
                    nc.vector.tensor_scalar(h_min[:, rows(t)], h[:, rows(t)], 0.0, None, ALU.min).then_inc(
                        min_ready, 1)

            def last_moments_of(pair):
                for t in pair:
                    dve.wait_ge(last_exp_ready, t + 1)
                    dve.wait_ge(last_x1_added, t + 1)
                    nc.vector.scalar_tensor_tensor(h[:, rows(t)], last_exp[:, rows(t)], -1.0, h[:, rows(t)],
                                                   ALU.add, ALU.add).then_inc(last_res_ready, 1)
                for t in pair:
                    dve.wait_ge(last_res_ready, t + 1)
                    nc.vector.bn_stats(stats[:, t, :], h[:, rows(t)]).then_inc(stats2_ready, 1)
                for t in pair:
                    dve.wait_ge(stats2_ready, LAST * IT + (t + 1))
                    nc.vector.bn_aggr(moments[:, t, :], stats[:, t, :]).then_inc(moments2_ready, 1)

            def last_norm_of(pair):
                dve.wait_ge(rstd2_ready, LAST + (pair[0] // 2 + 1))
                for t in pair:
                    nc.vector.tensor_scalar(h[:, rows(t)], h[:, rows(t)], moments[:, t, 0:1], rstd[:, t:t + 1],
                                            ALU.subtract, ALU.mult).then_inc(normed, 1)

            last_rows_of((0, 1))
            last_rows_of((2, 3))
            last_moments_of((0, 1))
            last_moments_of((2, 3))
            last_norm_of((0, 1))
            last_norm_of((2, 3))

            dve.wait_ge(wide_known, 1)
            with dve.If(dve.value_load(is_wide[0:1, 0:1], min_val=0, max_val=1) > 0):
                wide_rows()


def kernel(x, adj, L0_gnn_W, L0_gnn_b, L1_gnn_W, L1_gnn_a):
    import numpy as np
    import concourse.bacc as bacc
    from concourse.bass_utils import run_bass_kernel_spmd

    adj_t = np.asarray(adj).T.reshape(NT, P, NG, GI).transpose(2, 1, 0, 3).reshape(NG, P, NT * GI)
    arrays = {
        "x_tiles": np.asarray(x).reshape(NT, P, F).transpose(1, 0, 2),
        "adj_tiles": adj_t,
        "w0t": np.asarray(L0_gnn_W).T,
        "b0": np.asarray(L0_gnn_b).reshape(1, F),
        "w1": np.asarray(L1_gnn_W),
        "w1t": np.asarray(L1_gnn_W).T,
        "a_cols": np.asarray(L1_gnn_a).reshape(2, F).T,
    }
    arrays = {k: np.ascontiguousarray(v) for k, v in arrays.items()}
    nc = bacc.Bacc("TRN2", target_bir_lowering=False, num_devices=1)
    args = [nc.dram_tensor(k, v.shape, mybir.dt.from_np(v.dtype), kind="ExternalInput").ap()
            for k, v in arrays.items()]
    out = nc.dram_tensor("out_tiles", (P, NT, F), F32, kind="ExternalOutput").ap()
    build(nc, *args, out)
    r = run_bass_kernel_spmd(nc, [arrays], core_ids=[0])
    got = r.results[0]["out_tiles"]
    return np.ascontiguousarray(got.transpose(1, 0, 2).reshape(N, F))
```
